# Optimizing a Trainium2 kernel written in Bass

```python
import numpy as np
import jax
import jax.numpy as jnp

def _softmax(x, axis=-1):
    return jax.nn.softmax(x, axis=axis)

def _gelu(x):
    return jax.nn.gelu(x, approximate=True)

def _silu(x):
    return jax.nn.silu(x)

def _sigmoid(x):
    return jax.nn.sigmoid(x)

def _layernorm(x, axis=-1, eps=1e-05):
    m = jnp.mean(x, axis=axis, keepdims=True)
    v = jnp.var(x, axis=axis, keepdims=True)
    return (x - m) / jnp.sqrt(v + eps)

def _scatter_add(tgt, idx, src, axis=0):
    return tgt.at[idx].add(src)

def _segment_sum(src, seg, n):
    return jax.ops.segment_sum(src, seg, n)
kernel_name = 'mk_cond_seq_d4_seqx_r8_f50ac7'

def setup_inputs(seed: int=0):
    np.random.seed(seed)
    _w = jnp.asarray

    def _rec_inputs():
        import jax
        import jax.numpy as jnp
        _rk = jax.random.key(seed)
        x = -0.0002928 + 1 * jax.random.normal(jax.random.fold_in(_rk, 1), (2, 512, 128), jnp.float32)
        _lenS = 512 - jax.random.randint(jax.random.fold_in(_rk, 7), (2,), 0, max(1, 512 // 4) + 1, jnp.int32)
        _lenS2 = 512 - jax.random.randint(jax.random.fold_in(_rk, 8), (2,), 0, max(1, 512 // 4) + 1, jnp.int32)
        cond_1024 = 0.000887014 + 1.03683 * jax.random.normal(jax.random.fold_in(_rk, 11), (2, 128), jnp.float32)
        fside_BxSx3_0 = jax.random.uniform(jax.random.fold_in(_rk, 12), (2, 512, 3), jnp.float32, 0.0, 0.999943)
        return (x, cond_1024, fside_BxSx3_0)
    x, cond_1024, fside_BxSx3_0 = _rec_inputs()

    def _L0_cond_setup():
        import jax, jax.numpy as jnp
        import numpy as np
        HID = 128
        HEADS = 16
        HEAD_DIM = HID // HEADS
        ROPE_DIM = HEAD_DIM // 6 * 6
        HALF = ROPE_DIM // 3 // 2
        SWIGLU_HID = int(2 * (HID * 4) / 3)
        EPS = 1e-06
        THETA = 10000.0

        def rmsnorm(x, w, eps=EPS):
            xf = x.astype(jnp.float32)
            v = jnp.mean(xf * xf, axis=-1, keepdims=True)
            return w * (xf * jax.lax.rsqrt(v + eps)).astype(x.dtype)

        def modulate(x, shift, scale):
            return x * (1.0 + scale) + shift

        def rope_freqs():
            return 1.0 / THETA ** (jnp.arange(HALF, dtype=jnp.float32) / HALF)

        def apply_rope3d(q, k, positions):
            freqs = rope_freqs()
            ang = positions[..., :, None] * freqs
            ang = ang.reshape(ang.shape[0], ang.shape[1], -1)
            cos = jnp.cos(ang)[:, :, None, :]
            sin = jnp.sin(ang)[:, :, None, :]

            def rot(t):
                B, N, H, D = t.shape
                tr = t.reshape(B, N, H, D // 2, 2)
                t0, t1 = (tr[..., 0], tr[..., 1])
                out = jnp.stack([t0 * cos - t1 * sin, t0 * sin + t1 * cos], axis=-1)
                return out.reshape(B, N, H, D)
            return (rot(q), rot(k))
        key = jax.random.key(seed)
        ks = jax.random.split(key, 12)
        B, N = (2, 256)
        s = 0.02
        return {'x': jax.random.normal(ks[0], (B, N, HID), jnp.float32), 'c': jax.random.normal(ks[1], (B, HID), jnp.float32), 'positions': jax.random.uniform(ks[2], (B, N, 3), jnp.float32), 'norm1_w': jnp.ones((HID,), jnp.float32), 'qkv_w': jax.random.normal(ks[3], (3 * HID, HID), jnp.float32) * s, 'q_norm_w': jnp.ones((HEAD_DIM,), jnp.float32), 'k_norm_w': jnp.ones((HEAD_DIM,), jnp.float32), 'proj_w': jax.random.normal(ks[4], (HID, HID), jnp.float32) * s, 'proj_b': jnp.zeros((HID,), jnp.float32), 'norm2_w': jnp.ones((HID,), jnp.float32), 'w1': jax.random.normal(ks[5], (SWIGLU_HID, HID), jnp.float32) * s, 'w3': jax.random.normal(ks[6], (SWIGLU_HID, HID), jnp.float32) * s, 'w2': jax.random.normal(ks[7], (HID, SWIGLU_HID), jnp.float32) * s, 'ada_w': jax.random.normal(ks[8], (6 * HID, HID), jnp.float32) * s, 'ada_b': jnp.zeros((6 * HID,), jnp.float32)}
    _L0_cond_all = _L0_cond_setup()
    _L0_cond_in = {k: v for k, v in _L0_cond_all.items() if k in ('norm1_w', 'qkv_w', 'q_norm_w', 'k_norm_w', 'proj_w', 'proj_b', 'norm2_w', 'w1', 'w3', 'w2', 'ada_w', 'ada_b')}
    del _L0_cond_all

    def _L1_cond_setup():
        import jax, jax.numpy as jnp
        import numpy as np
        D = 128
        H = 16
        HD = 4 * D
        B, T = (4, 128)
        EPS = 1e-05

        def _layernorm(x, g, b):
            mu = jnp.mean(x, axis=-1, keepdims=True)
            var = jnp.mean(jnp.square(x - mu), axis=-1, keepdims=True)
            return (x - mu) * jax.lax.rsqrt(var + EPS) * g + b

        def _attention(x, Wqkv, Wproj, bproj):
            b, t, c = x.shape
            hd = c // H
            qkv = (x @ Wqkv).reshape(b, t, 3, H, hd).transpose(2, 0, 3, 1, 4)
            q, k, v = (qkv[0], qkv[1], qkv[2])
            scale = hd ** (-0.5)
            scores = jnp.einsum('bhqd,bhkd->bhqk', q, k) * scale
            causal = jnp.tril(jnp.ones((t, t), bool))
            scores = jnp.where(causal, scores, -jnp.inf)
            attn = jax.nn.softmax(scores, axis=-1)
            out = jnp.einsum('bhqk,bhkd->bhqd', attn, v)
            out = out.transpose(0, 2, 1, 3).reshape(b, t, c)
            return out @ Wproj + bproj
        key = jax.random.key(seed)
        ks = jax.random.split(key, 12)
        s = 0.02
        return {'x': jax.random.normal(ks[0], (B, T, D), jnp.float32), 'condition': jax.random.normal(ks[1], (B, D), jnp.float32), 'Wqkv': jax.random.normal(ks[2], (D, 3 * D), jnp.float32) * s, 'Wproj': jax.random.normal(ks[3], (D, D), jnp.float32) * s, 'bproj': jnp.zeros((D,), jnp.float32), 'W1': jax.random.normal(ks[4], (D, HD), jnp.float32) * s, 'b1': jnp.zeros((HD,), jnp.float32), 'W2': jax.random.normal(ks[5], (HD, D), jnp.float32) * s, 'b2': jnp.zeros((D,), jnp.float32), 'g1': jnp.ones((D,), jnp.float32), 'be1': jnp.zeros((D,), jnp.float32), 'g2': jnp.ones((D,), jnp.float32), 'be2': jnp.zeros((D,), jnp.float32), 'Wada': jax.random.normal(ks[6], (D, 6 * D), jnp.float32) * s, 'bada': jax.random.normal(ks[7], (6 * D,), jnp.float32) * s}
    _L1_cond_all = _L1_cond_setup()
    _L1_cond_in = {k: v for k, v in _L1_cond_all.items() if k in ('Wqkv', 'Wproj', 'bproj', 'W1', 'b1', 'W2', 'b2', 'g1', 'be1', 'g2', 'be2', 'Wada', 'bada')}
    del _L1_cond_all

    def _L2_cond_setup():
        import jax, jax.numpy as jnp
        import numpy as np
        D = 128
        H = 16
        HKV = 4
        HD = D // H
        REP = H // HKV
        DFF = 512
        B, N = (4, 256)
        EPS = 1e-05
        WSCALE = 0.02

        def _ln(x):
            m = jnp.mean(x, axis=-1, keepdims=True)
            v = jnp.mean(jnp.square(x - m), axis=-1, keepdims=True)
            return (x - m) * jax.lax.rsqrt(v + EPS)

        def _gqa_attn(h, wq, wk, wv, wo):
            b, n, d = h.shape
            q = (h @ wq.T).reshape(b, n, HKV, REP, HD)
            k = (h @ wk.T).reshape(b, n, HKV, HD)
            v = (h @ wv.T).reshape(b, n, HKV, HD)
            scores = jnp.einsum('bqgrh,bkgh->bgrqk', q, k) * (1.0 / np.sqrt(HD))
            a = jax.nn.softmax(scores, axis=-1)
            out = jnp.einsum('bgrqk,bkgh->bqgrh', a, v).reshape(b, n, d)
            return out @ wo.T

        def _mlp(h, w1, b1, w2, b2):
            h = jax.nn.gelu(h @ w1.T + b1, approximate=False)
            return h @ w2.T + b2
        key = jax.random.key(seed)
        ks = jax.random.split(key, 10)
        return {'x': jax.random.normal(ks[0], (B, N, D), jnp.float32), 'c': jax.random.normal(ks[1], (B, D), jnp.float32), 'wq': jax.random.normal(ks[2], (D, D), jnp.float32) * WSCALE, 'wk': jax.random.normal(ks[3], (HKV * HD, D), jnp.float32) * WSCALE, 'wv': jax.random.normal(ks[4], (HKV * HD, D), jnp.float32) * WSCALE, 'wo': jax.random.normal(ks[5], (D, D), jnp.float32) * WSCALE, 'w1': jax.random.normal(ks[6], (DFF, D), jnp.float32) * WSCALE, 'b1': jnp.zeros((DFF,), jnp.float32), 'w2': jax.random.normal(ks[7], (D, DFF), jnp.float32) * WSCALE, 'b2': jnp.zeros((D,), jnp.float32), 'wc': jax.random.normal(ks[8], (6 * D, D), jnp.float32) * WSCALE, 'bc': jnp.zeros((6 * D,), jnp.float32)}
    _L2_cond_all = _L2_cond_setup()
    _L2_cond_in = {k: v for k, v in _L2_cond_all.items() if k in ('wq', 'wk', 'wv', 'wo', 'w1', 'b1', 'w2', 'b2', 'wc', 'bc')}
    del _L2_cond_all

    def _L3_cond_setup():
        import jax, jax.numpy as jnp
        import numpy as np
        DIM = 128
        FF_MULT = 2
        EPS = 1e-06

        def _ln(x):
            mu = jnp.mean(x, axis=-1, keepdims=True)
            var = jnp.mean(jnp.square(x - mu), axis=-1, keepdims=True)
            return (x - mu) * jax.lax.rsqrt(var + EPS)
        key = jax.random.key(seed)
        ks = jax.random.split(key, 12)
        b, n, d = (4, 256, DIM)
        h = FF_MULT * d
        s = lambda fan_in: 1.0 / np.sqrt(fan_in)
        return {'x': jax.random.normal(ks[0], (b, n, d), jnp.float32), 't': jax.random.normal(ks[1], (b, d), jnp.float32), 'ada_w': jax.random.normal(ks[2], (d, 6 * d), jnp.float32) * s(d), 'ada_b': jnp.zeros((6 * d,), jnp.float32), 'ssm_w1': jax.random.normal(ks[3], (d, d), jnp.float32) * s(d), 'ssm_b1': jnp.zeros((d,), jnp.float32), 'ssm_w2': jax.random.normal(ks[4], (d, d), jnp.float32) * s(d), 'ssm_b2': jnp.zeros((d,), jnp.float32), 'ff_w1': jax.random.normal(ks[5], (d, h), jnp.float32) * s(d), 'ff_b1': jnp.zeros((h,), jnp.float32), 'ff_w2': jax.random.normal(ks[6], (h, d), jnp.float32) * s(h), 'ff_b2': jnp.zeros((d,), jnp.float32)}
    _L3_cond_all = _L3_cond_setup()
    _L3_cond_in = {k: v for k, v in _L3_cond_all.items() if k in ('ada_w', 'ada_b', 'ssm_w1', 'ssm_b1', 'ssm_w2', 'ssm_b2', 'ff_w1', 'ff_b1', 'ff_w2', 'ff_b2')}
    del _L3_cond_all
    return {'x': x, 'cond_1024': cond_1024, 'fside_BxSx3_0': fside_BxSx3_0, 'L0_cond_norm1_w': _L0_cond_in['norm1_w'], 'L0_cond_qkv_w': _L0_cond_in['qkv_w'], 'L0_cond_q_norm_w': _L0_cond_in['q_norm_w'], 'L0_cond_k_norm_w': _L0_cond_in['k_norm_w'], 'L0_cond_proj_w': _L0_cond_in['proj_w'], 'L0_cond_proj_b': _L0_cond_in['proj_b'], 'L0_cond_norm2_w': _L0_cond_in['norm2_w'], 'L0_cond_w1': _L0_cond_in['w1'], 'L0_cond_w3': _L0_cond_in['w3'], 'L0_cond_w2': _L0_cond_in['w2'], 'L0_cond_ada_w': _L0_cond_in['ada_w'], 'L0_cond_ada_b': _L0_cond_in['ada_b'], 'L1_cond_Wqkv': _L1_cond_in['Wqkv'], 'L1_cond_Wproj': _L1_cond_in['Wproj'], 'L1_cond_bproj': _L1_cond_in['bproj'], 'L1_cond_W1': _L1_cond_in['W1'], 'L1_cond_b1': _L1_cond_in['b1'], 'L1_cond_W2': _L1_cond_in['W2'], 'L1_cond_b2': _L1_cond_in['b2'], 'L1_cond_g1': _L1_cond_in['g1'], 'L1_cond_be1': _L1_cond_in['be1'], 'L1_cond_g2': _L1_cond_in['g2'], 'L1_cond_be2': _L1_cond_in['be2'], 'L1_cond_Wada': _L1_cond_in['Wada'], 'L1_cond_bada': _L1_cond_in['bada'], 'L2_cond_wq': _L2_cond_in['wq'], 'L2_cond_wk': _L2_cond_in['wk'], 'L2_cond_wv': _L2_cond_in['wv'], 'L2_cond_wo': _L2_cond_in['wo'], 'L2_cond_w1': _L2_cond_in['w1'], 'L2_cond_b1': _L2_cond_in['b1'], 'L2_cond_w2': _L2_cond_in['w2'], 'L2_cond_b2': _L2_cond_in['b2'], 'L2_cond_wc': _L2_cond_in['wc'], 'L2_cond_bc': _L2_cond_in['bc'], 'L3_cond_ada_w': _L3_cond_in['ada_w'], 'L3_cond_ada_b': _L3_cond_in['ada_b'], 'L3_cond_ssm_w1': _L3_cond_in['ssm_w1'], 'L3_cond_ssm_b1': _L3_cond_in['ssm_b1'], 'L3_cond_ssm_w2': _L3_cond_in['ssm_w2'], 'L3_cond_ssm_b2': _L3_cond_in['ssm_b2'], 'L3_cond_ff_w1': _L3_cond_in['ff_w1'], 'L3_cond_ff_b1': _L3_cond_in['ff_b1'], 'L3_cond_ff_w2': _L3_cond_in['ff_w2'], 'L3_cond_ff_b2': _L3_cond_in['ff_b2']}

def reference(x, cond_1024, fside_BxSx3_0, L0_cond_norm1_w, L0_cond_qkv_w, L0_cond_q_norm_w, L0_cond_k_norm_w, L0_cond_proj_w, L0_cond_proj_b, L0_cond_norm2_w, L0_cond_w1, L0_cond_w3, L0_cond_w2, L0_cond_ada_w, L0_cond_ada_b, L1_cond_Wqkv, L1_cond_Wproj, L1_cond_bproj, L1_cond_W1, L1_cond_b1, L1_cond_W2, L1_cond_b2, L1_cond_g1, L1_cond_be1, L1_cond_g2, L1_cond_be2, L1_cond_Wada, L1_cond_bada, L2_cond_wq, L2_cond_wk, L2_cond_wv, L2_cond_wo, L2_cond_w1, L2_cond_b1, L2_cond_w2, L2_cond_b2, L2_cond_wc, L2_cond_bc, L3_cond_ada_w, L3_cond_ada_b, L3_cond_ssm_w1, L3_cond_ssm_b1, L3_cond_ssm_w2, L3_cond_ssm_b2, L3_cond_ff_w1, L3_cond_ff_b1, L3_cond_ff_w2, L3_cond_ff_b2):
    import jax
    import jax.numpy as jnp

    def _L0_cond_ref(x, c, positions, norm1_w, qkv_w, q_norm_w, k_norm_w, proj_w, proj_b, norm2_w, w1, w3, w2, ada_w, ada_b):
        import jax, jax.numpy as jnp
        import numpy as np
        HID = 128
        HEADS = 16
        HEAD_DIM = HID // HEADS
        ROPE_DIM = HEAD_DIM // 6 * 6
        HALF = ROPE_DIM // 3 // 2
        SWIGLU_HID = int(2 * (HID * 4) / 3)
        EPS = 1e-06
        THETA = 10000.0

        def rmsnorm(x, w, eps=EPS):
            xf = x.astype(jnp.float32)
            v = jnp.mean(xf * xf, axis=-1, keepdims=True)
            return w * (xf * jax.lax.rsqrt(v + eps)).astype(x.dtype)

        def modulate(x, shift, scale):
            return x * (1.0 + scale) + shift

        def rope_freqs():
            return 1.0 / THETA ** (jnp.arange(HALF, dtype=jnp.float32) / HALF)

        def apply_rope3d(q, k, positions):
            freqs = rope_freqs()
            ang = positions[..., :, None] * freqs
            ang = ang.reshape(ang.shape[0], ang.shape[1], -1)
            cos = jnp.cos(ang)[:, :, None, :]
            sin = jnp.sin(ang)[:, :, None, :]

            def rot(t):
                B, N, H, D = t.shape
                tr = t.reshape(B, N, H, D // 2, 2)
                t0, t1 = (tr[..., 0], tr[..., 1])
                out = jnp.stack([t0 * cos - t1 * sin, t0 * sin + t1 * cos], axis=-1)
                return out.reshape(B, N, H, D)
            return (rot(q), rot(k))
        B, N, C = x.shape
        H, D = (HEADS, HEAD_DIM)
        mod = (c @ ada_w.T + ada_b)[:, None, :]
        sh_msa, sc_msa, g_msa, sh_mlp, sc_mlp, g_mlp = jnp.split(mod, 6, axis=-1)
        h = modulate(rmsnorm(x, norm1_w), sh_msa, sc_msa)
        qkv = (h @ qkv_w.T).reshape(B, N, 3, H, D)
        q, k, v = (qkv[:, :, 0], qkv[:, :, 1], qkv[:, :, 2])
        q = rmsnorm(q, q_norm_w)
        k = rmsnorm(k, k_norm_w)
        q_r, k_r = apply_rope3d(q[..., :ROPE_DIM], k[..., :ROPE_DIM], positions)
        q = jnp.concatenate([q_r, q[..., ROPE_DIM:]], axis=-1)
        k = jnp.concatenate([k_r, k[..., ROPE_DIM:]], axis=-1)
        scale = D ** (-0.5)
        attn = jnp.einsum('bnhd,bmhd->bhnm', q, k) * scale
        attn = jax.nn.softmax(attn, axis=-1)
        o = jnp.einsum('bhnm,bmhd->bnhd', attn, v).reshape(B, N, C)
        o = o @ proj_w.T + proj_b
        x = x + g_msa * o
        h2 = modulate(rmsnorm(x, norm2_w), sh_mlp, sc_mlp)
        ff = jax.nn.silu(h2 @ w1.T) * (h2 @ w3.T) @ w2.T
        x = x + g_mlp * ff
        return x

    def _L1_cond_ref(x, condition, Wqkv, Wproj, bproj, W1, b1, W2, b2, g1, be1, g2, be2, Wada, bada):
        import jax, jax.numpy as jnp
        import numpy as np
        D = 128
        H = 16
        HD = 4 * D
        B, T = (4, 128)
        EPS = 1e-05

        def _layernorm(x, g, b):
            mu = jnp.mean(x, axis=-1, keepdims=True)
            var = jnp.mean(jnp.square(x - mu), axis=-1, keepdims=True)
            return (x - mu) * jax.lax.rsqrt(var + EPS) * g + b

        def _attention(x, Wqkv, Wproj, bproj):
            b, t, c = x.shape
            hd = c // H
            qkv = (x @ Wqkv).reshape(b, t, 3, H, hd).transpose(2, 0, 3, 1, 4)
            q, k, v = (qkv[0], qkv[1], qkv[2])
            scale = hd ** (-0.5)
            scores = jnp.einsum('bhqd,bhkd->bhqk', q, k) * scale
            causal = jnp.tril(jnp.ones((t, t), bool))
            scores = jnp.where(causal, scores, -jnp.inf)
            attn = jax.nn.softmax(scores, axis=-1)
            out = jnp.einsum('bhqk,bhkd->bhqd', attn, v)
            out = out.transpose(0, 2, 1, 3).reshape(b, t, c)
            return out @ Wproj + bproj
        mod = jax.nn.silu(condition) @ Wada + bada
        sh_a, sc_a, gt_a, sh_m, sc_m, gt_m = jnp.split(mod, 6, axis=1)
        xn = _layernorm(x, g1, be1)
        xm = xn * (1.0 + sc_a[:, None, :]) + sh_a[:, None, :]
        x = x + gt_a[:, None, :] * _attention(xm, Wqkv, Wproj, bproj)
        xn = _layernorm(x, g2, be2)
        xm = xn * (1.0 + sc_m[:, None, :]) + sh_m[:, None, :]
        h = jax.nn.gelu(xm @ W1 + b1, approximate=False)
        x = x + gt_m[:, None, :] * (h @ W2 + b2)
        return x

    def _L2_cond_ref(x, c, wq, wk, wv, wo, w1, b1, w2, b2, wc, bc):
        import jax, jax.numpy as jnp
        import numpy as np
        D = 128
        H = 16
        HKV = 4
        HD = D // H
        REP = H // HKV
        DFF = 512
        B, N = (4, 256)
        EPS = 1e-05
        WSCALE = 0.02

        def _ln(x):
            m = jnp.mean(x, axis=-1, keepdims=True)
            v = jnp.mean(jnp.square(x - m), axis=-1, keepdims=True)
            return (x - m) * jax.lax.rsqrt(v + EPS)

        def _gqa_attn(h, wq, wk, wv, wo):
            b, n, d = h.shape
            q = (h @ wq.T).reshape(b, n, HKV, REP, HD)
            k = (h @ wk.T).reshape(b, n, HKV, HD)
            v = (h @ wv.T).reshape(b, n, HKV, HD)
            scores = jnp.einsum('bqgrh,bkgh->bgrqk', q, k) * (1.0 / np.sqrt(HD))
            a = jax.nn.softmax(scores, axis=-1)
            out = jnp.einsum('bgrqk,bkgh->bqgrh', a, v).reshape(b, n, d)
            return out @ wo.T

        def _mlp(h, w1, b1, w2, b2):
            h = jax.nn.gelu(h @ w1.T + b1, approximate=False)
            return h @ w2.T + b2
        cond = jax.nn.silu(c) @ wc.T + bc
        sh1, sc1, g1, sh2, sc2, g2 = jnp.split(cond, 6, axis=-1)
        sh1, sc1, g1 = (sh1[:, None], sc1[:, None], g1[:, None])
        sh2, sc2, g2 = (sh2[:, None], sc2[:, None], g2[:, None])
        h = _ln(x) * (1.0 + sc1) + sh1
        x = x + g1 * _gqa_attn(h, wq, wk, wv, wo)
        h = _ln(x) * (1.0 + sc2) + sh2
        x = x + g2 * _mlp(h, w1, b1, w2, b2)
        return x

    def _L3_cond_ref(x, t, ada_w, ada_b, ssm_w1, ssm_b1, ssm_w2, ssm_b2, ff_w1, ff_b1, ff_w2, ff_b2):
        import jax, jax.numpy as jnp
        import numpy as np
        DIM = 128
        FF_MULT = 2
        EPS = 1e-06

        def _ln(x):
            mu = jnp.mean(x, axis=-1, keepdims=True)
            var = jnp.mean(jnp.square(x - mu), axis=-1, keepdims=True)
            return (x - mu) * jax.lax.rsqrt(var + EPS)
        emb = jnp.dot(jax.nn.silu(t), ada_w) + ada_b
        shift_msa, scale_msa, gate_msa, shift_mlp, scale_mlp, gate_mlp = jnp.split(emb, 6, axis=-1)
        norm = _ln(x) * (1.0 + scale_msa[:, None]) + shift_msa[:, None]
        h = jax.nn.gelu(jnp.dot(norm, ssm_w1) + ssm_b1, approximate=False)
        ssm_out = jnp.dot(h, ssm_w2) + ssm_b2
        x = x + gate_msa[:, None] * ssm_out
        norm2 = _ln(x) * (1.0 + scale_mlp[:, None]) + shift_mlp[:, None]
        hf = jax.nn.gelu(jnp.dot(norm2, ff_w1) + ff_b1, approximate=True)
        ff_out = jnp.dot(hf, ff_w2) + ff_b2
        x = x + gate_mlp[:, None] * ff_out
        return x
    x = _L0_cond_ref(x, cond_1024, fside_BxSx3_0, L0_cond_norm1_w, L0_cond_qkv_w, L0_cond_q_norm_w, L0_cond_k_norm_w, L0_cond_proj_w, L0_cond_proj_b, L0_cond_norm2_w, L0_cond_w1, L0_cond_w3, L0_cond_w2, L0_cond_ada_w, L0_cond_ada_b)
    x = _L1_cond_ref(x, cond_1024, L1_cond_Wqkv, L1_cond_Wproj, L1_cond_bproj, L1_cond_W1, L1_cond_b1, L1_cond_W2, L1_cond_b2, L1_cond_g1, L1_cond_be1, L1_cond_g2, L1_cond_be2, L1_cond_Wada, L1_cond_bada)
    x = _L2_cond_ref(x, cond_1024, L2_cond_wq, L2_cond_wk, L2_cond_wv, L2_cond_wo, L2_cond_w1, L2_cond_b1, L2_cond_w2, L2_cond_b2, L2_cond_wc, L2_cond_bc)
    x = _L3_cond_ref(x, cond_1024, L3_cond_ada_w, L3_cond_ada_b, L3_cond_ssm_w1, L3_cond_ssm_b1, L3_cond_ssm_w2, L3_cond_ssm_b2, L3_cond_ff_w1, L3_cond_ff_b1, L3_cond_ff_w2, L3_cond_ff_b2)
    return x

_drawn_inputs = setup_inputs


def setup_inputs(seed=0):
    import zlib

    import numpy as np

    out = dict(_drawn_inputs(seed))
    spreads = {'L0_cond_norm1_w': (1.0, 0.6),
     'L0_cond_q_norm_w': (1.0, 0.6),
     'L0_cond_k_norm_w': (1.0, 0.6),
     'L0_cond_proj_b': (0.0, 0.334),
     'L0_cond_norm2_w': (1.0, 0.6),
     'L0_cond_ada_b': (0.0, 0.732),
     'L1_cond_bproj': (0.0, 2.0),
     'L1_cond_b1': (0.0, 0.8),
     'L1_cond_b2': (0.0, 2.0),
     'L1_cond_g1': (1.0, 0.6),
     'L1_cond_be1': (0.0, 0.8),
     'L1_cond_g2': (1.0, 0.6),
     'L1_cond_be2': (0.0, 0.8),
     'L2_cond_b1': (0.0, 0.8),
     'L2_cond_b2': (0.0, 2.0),
     'L2_cond_bc': (0.0, 0.8),
     'L3_cond_ada_b': (0.0, 0.8),
     'L3_cond_ssm_b1': (0.0, 2.0),
     'L3_cond_ssm_b2': (0.0, 0.8),
     'L3_cond_ff_b1': (0.0, 2.0),
     'L3_cond_ff_b2': (0.0, 2.0)}
    factors = {'fside_BxSx3_0': 8.0,
     'L0_cond_qkv_w': 8.0,
     'L0_cond_proj_w': 8.0,
     'L0_cond_w1': 8.0,
     'L0_cond_w3': 8.0,
     'L0_cond_w2': 8.0,
     'L1_cond_Wqkv': 8.0,
     'L1_cond_Wproj': 8.0,
     'L1_cond_W1': 7.781,
     'L1_cond_W2': 7.172,
     'L1_cond_Wada': 2.998,
     'L1_cond_bada': 8.0,
     'L2_cond_wq': 8.0,
     'L2_cond_wk': 8.0,
     'L2_cond_wv': 8.0,
     'L2_cond_wo': 8.0,
     'L2_cond_w1': 6.75,
     'L2_cond_w2': 6.164,
     'L2_cond_wc': 3.527,
     'L3_cond_ssm_w1': 3.112,
     'L3_cond_ff_w1': 3.415,
     'L3_cond_ff_w2': 2.973}
    for name, (base, spread) in spreads.items():
        noise = np.random.default_rng([zlib.crc32(name.encode()), seed]).standard_normal(out[name].shape)
        drawn = base * np.exp(spread * noise) if base else spread * noise
        out[name] = jnp.asarray(drawn.astype(out[name].dtype))
    for name, factor in factors.items():
        out[name] = (out[name] * factor).astype(out[name].dtype)
    return out
```

```python
from contextlib import ExitStack

import concourse.bass as bass
from concourse import mybir

B, N, D = 2, 512, 128
LAYERS = 4
ATT_LAYERS = 3
H, HD = 16, 8
R = 4
GROUPS = H // R
TT = N // 128
TERMS = 9
TERM_ROWS = TERMS * HD
MAX_ROWS = 3
ROWS = TERM_ROWS + MAX_ROWS
VW = 32
SCALE = float(HD) ** -0.5
NEG = -1e30
HID0 = 341
HID_TILES = [3, 4, 4, 2]
EPS = [1e-6, 1e-5, 1e-5, 1e-6]
CAUSAL = [False, True, False]
BIAS_ROWS = {(0, 0): 0, (1, 0): 1, (1, 1): 2, (2, 1): 3, (3, 0): 4, (3, 1): 5}
GATE_ROW0 = len(BIAS_ROWS)
QKW0 = (GATE_ROW0 + 2 * LAYERS) * D
ROW_VECS = QKW0 + 2 * D
MODB0, NW0, NB0, HB0 = 0, 16, 24, 32
HID_BIAS = {1: HB0, 2: HB0 + 4, 3: HB0 + 9}
SSM_BIAS = HB0 + 8
COL_VECS = HB0 + 11

LAG = 6
LEAD = 6
ATT_TICKS = GROUPS * TT
N_ATT = ATT_LAYERS * B
TICKS = N_ATT * ATT_TICKS
Q = 4


def make_plan():
    plan = {}

    def put(point, *stage):
        plan.setdefault(point, []).append(stage)
        if stage[0] == "norm" and (stage[1], stage[3]) in BIAS_ROWS:
            if stage[1]:
                put(point, "bias", *stage[1:])
        return point

    def pre(p, l, b, gap):
        p = put(p + gap, "hT", l, b, 0)
        if l == 0:
            p = put(p + gap, "qk_rows", l, b)
            p = put(p + 2 * gap, "qk_scale", l, b)
            put(p + 2, "v", l, b)
            p = put(p + 2 * gap, "rope", l, b)
            p = put(p + 2 * gap, "q", l, b)
            p = put(p, "k", l, b)
        else:
            p = put(p + gap, "q", l, b)
            p = put(p, "k", l, b)
        p = put(p + 1, "q_mid", l, b)
        p = put(p, "k_mid", l, b)
        if l:
            p = put(p + 2, "v", l, b)
        p = put(p, "terms", l, b)
        return p

    def mlp(p, l, b, gap):
        if l == 0:
            for i in range(HID_TILES[0]):
                p = put(p + 3, "swiglu", l, b, i)
        else:
            p = put(p + gap, "up", l, b)
        for tt in range(TT):
            p = put(p + 1, "down", l, b, tt)
        return p

    def last_block(p, b):
        p = put(p + 2, "norm", 3, b, 0)
        p = put(p + 2, "hT", 3, b, 0)
        p = put(p + 2, "ssm", 3, b)
        p = put(p + 2, "ssm_out", 3, b)
        p = put(p + 2, "norm", 3, b, 1)
        p = put(p + 2, "hT", 3, b, 1)
        p = mlp(p, 3, b, 2)
        put(p, "store", b)

    put(0, "modcol", 0)
    put(1, "norm", 0, 0, 0)
    put(4, "spread")
    pre(2, 0, 0, 2)
    base = Q * LEAD
    put(base, "norm", 0, 1, 0)
    pre(base, 0, 1, 3)
    put(base + 22, "gate", 0)
    for b in range(B):
        put(base + 23, "bias", 0, b, 0)
    for l in range(1, LAYERS):
        put(base + 14 + 14 * l, "modcol", l)
        put(base + 16 + 14 * l, "gate", l)
    for a in range(N_ATT):
        l, b = divmod(a, B)
        for g in range(GROUPS):
            G = a * GROUPS + g
            put(base + Q * (4 * G + 4) + 2, "max_rows", G)
            p = put(base + Q * (4 * G + LAG + 5), "fold", G)
        p = put(p + 1, "oT", l, b)
        p = put(p + 2, "out", l, b)
        p = put(p + 1, "norm", l, b, 1)
        p = put(p + 2, "hT", l, b, 1)
        p = mlp(p, l, b, 1)
        if l + 1 < ATT_LAYERS:
            p = put(p + 1, "norm", l + 1, b, 0)
            pre(p, l + 1, b, 1)
        else:
            last_block(p, b)
    return plan


PLAN = make_plan()
LAST_POINT = max(max(PLAN), Q * (LEAD + TICKS + LAG + 1)) + 1


def stages(name=None):
    out = [s for p in sorted(PLAN) for s in PLAN[p]]
    return [s[1:] for s in out if s[0] == name] if name else out


def spare_uses():
    out = []
    for s in stages():
        if s[0] in ("modcol", "gate", "fold", "max_rows", "hT", "oT", "out", "v", "q", "k", "ssm", "ssm_out"):
            out.append(s)
        elif s[0] == "qk_rows":
            out += [("q_rows", *s[1:]), ("k_rows", *s[1:])]
        elif s[0] == "swiglu":
            out += [("gate_half", *s[1:]), ("up_half", *s[1:])]
        elif s[0] == "up":
            out += [("up", *s[1:], i) for i in range(HID_TILES[s[1]])]
        elif s[0] == "down" and s[3] == 0:
            out.append(("down", *s[1:3]))
    return out


SPARE = {s: n for n, s in enumerate(spare_uses())}
assert len(SPARE) == len(spare_uses())


def order(name):
    return {s: n for n, s in enumerate(stages(name))}


NORMS = order("norm")
HTS = order("hT")
MODS = order("modcol")
BIASED = stages("bias")


def hid_rows(l, i):
    return min(128, HID0 - 128 * i) if l == 0 else 128


def program(nc, t_in, out):
    f32, bf16, i32 = mybir.dt.float32, mybir.dt.bfloat16, mybir.dt.int32
    ALU, ACT, AX = mybir.AluOpType, mybir.ActivationFunctionType, mybir.AxisListType
    ctx = ExitStack()
    with ctx:
        def sb(name, shape, dt=f32):
            return ctx.enter_context(nc.sbuf_tensor(name, shape, dt))

        def sem(name):
            return ctx.enter_context(nc.semaphore(name))

        wqkv = [sb(f"wqkv{l}", [128, 3, D]) for l in range(ATT_LAYERS)]
        wout = [sb(f"wout{l}", [128, D]) for l in range(LAYERS)]
        wada = [sb(f"wada{l}", [128, 6, D]) for l in range(LAYERS)]
        wup0 = sb("wup0", [128, 2, HID0])
        wup = [None] + [sb(f"wup{l}", [128, HID_TILES[l] * 128]) for l in range(1, LAYERS)]
        wssm = sb("wssm", [128, D])
        wdown = [sb(f"wdown{l}", [128, HID_TILES[l], D]) for l in range(LAYERS)]
        wout_g = [[sb(f"wout_g{l}", [128, D]), wout[l]] for l in range(LAYERS)]
        wdown_g = [[sb(f"wdown_g{l}", [128, HID_TILES[l], D]), wdown[l]] for l in range(LAYERS)]
        bias_g = {k: sb(f"bias_g{k[0]}{k[1]}", [128, B, D]) for k in BIAS_ROWS}
        col = sb("col", [128, COL_VECS])
        row = sb("row", [128, ROW_VECS])
        cond = sb("cond", [128, B])
        cond_t = sb("cond_t", [128, B])
        cond_silu = sb("cond_silu", [128, B])
        cond_wide = sb("cond_wide", [128, 2, B, 128])
        mod = sb("mod", [128, LAYERS, 2, 2, B])
        mod_scale = sb("mod_scale", [128, LAYERS, 2, B])
        mod_shift = sb("mod_shift", [128, LAYERS, 2, B])
        gates = sb("gates", [128, 2, B, D])
        pos = sb("pos", [128, B * TT * 3])
        turns = sb("turns", [128, B * TT * 3])
        angle = sb("angle", [128, B * TT * 3])
        angle_c = sb("angle_c", [128, B * TT * 3])
        sin3 = sb("sin3", [128, B, TT, 3])
        cos3 = sb("cos3", [128, B, TT, 3])
        sin_w = sb("sin_w", [128, B, 2 * TT, 3 * H])
        cos_w = sb("cos_w", [128, B, 2 * TT, 3 * H])
        ident = sb("ident", [128, 128])
        ident16 = sb("ident16", [128, 128], bf16)
        mask_s = sb("mask_s", [128, 128], bf16)
        mask_t = sb("mask_t", [128, 128], bf16)
        minus_half = sb("minus_half", [128, 2 * TT * H])
        x = [sb(f"x{b}", [128, TT, D]) for b in range(B)]
        bn = sb("bn", [128, TT, 6])
        mv = sb("mv", [128, TT, 2])
        msq = sb("msq", [128, TT])
        ve = sb("ve", [128, TT])
        rstd = sb("rstd", [128, TT])
        xn = sb("xn", [128, TT, D])
        hT = sb("hT", [128, N])
        hidden = sb("hidden", [128, 4, N])
        tanh_a = sb("tanh_a", [128, N])
        qk = sb("qk", [128, 2, N])
        ss = sb("ss", [128, 2 * TT * H])
        qk_rs = sb("qk_rs", [128, 2 * TT * H])
        parts = [sb(f"{n}_parts", [128, 3, N], bf16) for n in "qk"]
        rest = [qk[:, 0, :], qk[:, 1, :]]
        qx = [sb(f"qx{b}", [128, H, N], bf16) for b in range(B)]
        kx = [sb(f"kx{b}", [128, H, N], bf16) for b in range(B)]
        vx = [sb(f"vx{b}", [128, TT * H, VW]) for b in range(B)]
        nmax = sb("nmax", [128, 2, TT * R])
        nrest = sb("nrest", [128, 2, TT * R])
        nmax_parts = sb("nmax_parts", [128, 2, TT, 3, R], bf16)
        max_rows = sb("max_rows", [3 * R, 2, N], bf16)
        probs = sb("probs", [128, 8, N])
        o_sb = sb("o_sb", [128, 2, N])
        rden = sb("rden", [128, TT, R])
        o_rows = sb("o_rows", [128, TT, D])
        oT = sb("oT", [128, N])

        smax = [ctx.enter_context(nc.psum_tensor(f"smax{i}", [128, N], f32)) for i in range(2)]
        st = [ctx.enter_context(nc.psum_tensor(f"st{i}", [128, N], f32)) for i in range(3)]
        o_acc = ctx.enter_context(nc.psum_tensor("o_acc", [128, N], f32))
        spare = [ctx.enter_context(nc.psum_tensor(f"spare{i}", [128, N], f32)) for i in range(2)]

        ld_x = sem("ld_x")
        ld_cond = sem("ld_cond")
        ld_small = sem("ld_small")
        ld_ada = [sem(f"ld_ada{l}") for l in range(LAYERS)]
        ld_qkv = [sem(f"ld_qkv{l}") for l in range(ATT_LAYERS)]
        ld_w = [sem(f"ld_w{l}") for l in range(LAYERS)]
        identity_ready = sem("identity_ready")
        consts_ready = sem("consts_ready")
        ones_ready = sem("ones_ready")
        pool_step = sem("pool_step")
        dve_step = sem("dve_step")
        act_step = sem("act_step")
        cond_tanh = sem("cond_tanh")
        cond_ready = sem("cond_ready")
        mod_ready = sem("mod_ready")
        gated_ready = sem("gated_ready")
        angles_ready = sem("angles_ready")
        sines_ready = sem("sines_ready")
        spare_full = [sem(f"spare_full{i}") for i in range(2)]
        spare_free = [sem(f"spare_free{i}") for i in range(2)]
        xb_ready = sem("xb_ready")
        var_ready = sem("var_ready")
        rstd_ready = sem("rstd_ready")
        xn_ready = sem("xn_ready")
        tanh_ready = sem("tanh_ready")
        sq_ready = sem("sq_ready")
        ss_ready = sem("ss_ready")
        qk_rs_ready = sem("qk_rs_ready")
        qk_ready = sem("qk_ready")
        hi_ready = sem("hi_ready")
        mid_ready = sem("mid_ready")
        lo_ready = sem("lo_ready")
        sp_terms = [sem(f"sp_terms{b}") for b in range(B)]
        pool_terms = [sem(f"pool_terms{b}") for b in range(B)]
        smax_full = sem("smax_full")
        smax_free = sem("smax_free")
        nmax_ready = sem("nmax_ready")
        max_loaded = [sem(f"max_loaded{i}") for i in range(2)]
        st_full = sem("st_full")
        exp_done = sem("exp_done")
        pv_done = sem("pv_done")
        o_ready = sem("o_ready")
        stored = sem("stored")

        W_LOADS = [4, 3, 3, 4]

        def bank(*use):
            return spare[SPARE[use] % 2]

        def wait_full(eng, *use):
            n = SPARE[use]
            eng.wait_ge(spare_full[n % 2], n // 2 + 1)

        def full(*use):
            return spare_full[SPARE[use] % 2]

        def free(*use):
            return spare_free[SPARE[use] % 2]

        def wait_taken(eng, *use):
            n = SPARE[use]
            eng.wait_ge(spare_free[n % 2], n // 2 + 1)

        def wait_free(pe, *use):
            n = SPARE[use]
            if n >= 2:
                pe.wait_ge(spare_free[n % 2], n // 2)

        def att(a):
            l, b = divmod(a, B)
            return l, b

        def max_keys(l, qt):
            return 128 * (qt + 1) if CAUSAL[l] else N

        def first_query(l, kt):
            return 128 * kt if CAUSAL[l] else 0

        def max_tick(tick, T):
            t = tick - LEAD
            return (t // ATT_TICKS, t // TT % GROUPS, t % TT, t) if 0 <= t < TICKS else None

        def prob_tick(tick):
            return max_tick(tick - LAG, None)

        def pv_tick(tick):
            return max_tick(tick - LAG - 1, None)

        block = ctx.enter_context(nc.Block())

        @block.sync
        def _(sp):
            sp.dma_start(x[0][:, :, :], t_in["x"][0].rearrange("(t p) f -> p t f", p=128)).then_inc(ld_x, 16)
            sp.dma_start(wada[0][:, :, :], t_in["wada0"].rearrange("p (c f) -> p c f", f=D)).then_inc(ld_ada[0], 16)
            sp.dma_start(row[:, :], bass.AP(tensor=t_in["row_vecs"].tensor, offset=0,
                                               ap=[[0, 128], [1, ROW_VECS]])).then_inc(ld_small, 16)
            sp.dma_start(x[1][:, :, :], t_in["x"][1].rearrange("(t p) f -> p t f", p=128)).then_inc(ld_x, 16)
            sp.dma_start(wout[0][:, :], t_in["wout0"]).then_inc(ld_w[0], 16)
            sp.dma_start(wup0[:, :, :], t_in["wup0"].rearrange("p (c f) -> p c f", f=HID0)).then_inc(ld_w[0], 16)
            sp.dma_start(wdown[0][:, 0:2, :], t_in["wdown0"][0:256, :].rearrange("(t p) f -> p t f", p=128)).then_inc(ld_w[0], 16)
            sp.dma_start(wdown[0][0:HID0 - 256, 2, :], t_in["wdown0"][256:HID0, :]).then_inc(ld_w[0], 16)

            def load_layer(l):
                sp.dma_start(wada[l][:, :, :], t_in[f"wada{l}"].rearrange("p (c f) -> p c f", f=D)).then_inc(ld_ada[l], 16)
                if l < ATT_LAYERS:
                    sp.dma_start(wqkv[l][:, :, :], t_in[f"wqkv{l}"].rearrange("p (c f) -> p c f", f=D)).then_inc(ld_qkv[l], 16)
                else:
                    sp.dma_start(wssm[:, :], t_in["wssm"]).then_inc(ld_w[l], 16)
                sp.dma_start(wout[l][:, :], t_in[f"wout{l}"]).then_inc(ld_w[l], 16)
                sp.dma_start(wup[l][:, :], t_in[f"wup{l}"]).then_inc(ld_w[l], 16)
                sp.dma_start(wdown[l][:, :, :], t_in[f"wdown{l}"].rearrange("(t p) f -> p t f", p=128)).then_inc(ld_w[l], 16)

            def max_rows_out(G):
                a, g = divmod(G, GROUPS)
                wait_taken(sp, "max_rows", G)
                sp.dma_start(qx[att(a)[1]][TERM_ROWS:ROWS, R * g:R * g + R, :],
                             max_rows[:, G % 2, :]).then_inc(max_loaded[G % 2], 16)

            def terms_out(l, b):
                n = 2 * (l * B + b)
                for i, made in enumerate((hi_ready, mid_ready, lo_ready)):
                    sp.wait_ge(made, n + 1)
                    for j in range(3):
                        r0 = HD * (3 * i + j)
                        sp.dma_start(qx[b][r0:r0 + HD, :, :], parts[0][:, i, :]).then_inc(sp_terms[b], 16)
                sp.wait_ge(lo_ready, n + 2)
                sp.wait_ge(ones_ready, b + 1)
                for i in range(3):
                    r0 = HD * (3 * i + 2)
                    sp.dma_start(kx[b][r0:r0 + HD, :, :], parts[1][:, 2, :]).then_inc(sp_terms[b], 16)

            loads = {Q * LEAD: 1, Q * LEAD + 1: 2, Q * LEAD + 2: 3}
            for p in range(LAST_POINT):
                if p in loads:
                    load_layer(loads[p])
                for s in PLAN.get(p, []):
                    if s[0] == "max_rows":
                        max_rows_out(s[1])
                    elif s[0] == "terms":
                        terms_out(*s[1:])
                    elif s[0] == "store":
                        b = s[1]
                        wait_taken(sp, "down", 3, b)
                        sp.dma_start(out[b].rearrange("(t p) f -> p t f", p=128), x[b][:, :, :]).then_inc(stored, 16)
            sp.wait_ge(stored, 16 * B)

        @block.gpsimd
        def _(pool):
            pool.memset(minus_half[:, :], -0.5)
            pool.memset(ident[:, :], 0.0)
            pool.memset(ident16[:, :], 0.0)
            pool.memset(mask_s[:, :], 0.0)
            pool.memset(mask_t[:, :], 0.0).then_inc(pool_step, 1)
            pool.wait_ge(pool_step, 1)
            pool.affine_select(out=ident[:, :], in_=ident[:, :], compare_op=ALU.not_equal, fill=1.0,
                               base=0, pattern=[[-1, 128]], channel_multiplier=1).then_inc(identity_ready, 1)
            pool.affine_select(out=ident16[:, :], in_=ident16[:, :], compare_op=ALU.not_equal, fill=1.0,
                               base=0, pattern=[[-1, 128]], channel_multiplier=1)
            pool.affine_select(out=mask_s[:, :], in_=mask_s[:, :], compare_op=ALU.is_ge, fill=NEG,
                               base=0, pattern=[[-1, 128]], channel_multiplier=1)
            pool.affine_select(out=mask_t[:, :], in_=mask_t[:, :], compare_op=ALU.is_ge, fill=NEG,
                               base=0, pattern=[[1, 128]], channel_multiplier=-1).then_inc(consts_ready, 1)
            for b in range(B):
                pool.memset(vx[b][:, :, :], 0.0).then_inc(pool_step, 1)
                pool.wait_ge(pool_step, 2 + b)
                pool.memset(vx[b][:, :, HD:HD + 1], 1.0).then_inc(consts_ready, 1)

            def gated(l):
                wait_taken(pool, "gate", l)
                pool.wait_ge(ld_w[l], 16 * W_LOADS[l])
                if l == 0:
                    pool.wait_ge(ld_small, 16 * 4)
                last = None
                for b in range(B):
                    pool.tensor_tensor(wout_g[l][b][:, :], wout[l][:, :], gates[:, 0, b, :], ALU.mult)
                    for i in range(HID_TILES[l]):
                        k = hid_rows(l, i)
                        last = pool.tensor_tensor(wdown_g[l][b][0:k, i, :], wdown[l][0:k, i, :],
                                                  gates[0:k, 1, b, :], ALU.mult)
                for w in range(2):
                    if (l, w) in BIAS_ROWS:
                        r = BIAS_ROWS[(l, w)] * D
                        for b in range(B):
                            last = pool.tensor_tensor(bias_g[(l, w)][:, b, :], row[:, r:r + D], gates[:, w, b, :], ALU.mult)
                last.then_inc(gated_ready, 1)

            def add_bias(u, n):
                l, b, w = u
                pool.wait_ge(gated_ready, l + 1)
                pool.wait_ge(xn_ready, n + 1)
                pool.tensor_tensor(x[b][:, :, :], x[b][:, :, :],
                                   bias_g[(l, w)][:, b:b + 1, :].to_broadcast([128, TT, D]), ALU.add).then_inc(xb_ready, 1)

            def k_terms(l, b):
                n = 2 * (l * B + b)
                pool.wait_ge(ones_ready, b + 1)
                for j, made in enumerate((hi_ready, mid_ready)):
                    pool.wait_ge(made, n + 2)
                    for i in range(3):
                        r0 = HD * (3 * i + j)
                        pool.dma_start(kx[b][r0:r0 + HD, :, :], parts[1][:, j, :]).then_inc(pool_terms[b], 16)

            for p in range(LAST_POINT):
                for s in PLAN.get(p, []):
                    if s[0] == "norm":
                        pool.wait_ge(var_ready, NORMS[s[1:]] + 1)
                        pool.tensor_tensor(rstd[:, :], ve[:, :], minus_half[:, 0:TT], ALU.pow).then_inc(rstd_ready, 1)
                    elif s[0] == "qk_scale":
                        pool.wait_ge(ss_ready, s[2] + 1)
                        pool.tensor_tensor(qk_rs[:, :], ss[:, :], minus_half[:, :], ALU.pow).then_inc(qk_rs_ready, 1)
                    elif s[0] == "gate":
                        gated(s[1])
                    elif s[0] in ("q_mid", "k_mid"):
                        i = int(s[0] == "k_mid")
                        n = 2 * (s[1] * B + s[2]) + i
                        pool.wait_ge(mid_ready, n + 1)
                        pool.tensor_tensor(parts[i][:, 2, :], rest[i], parts[i][:, 1, :],
                                           ALU.subtract).then_inc(lo_ready, 1)
                    elif s[0] == "terms":
                        k_terms(*s[1:])
                    elif s[0] == "bias":
                        add_bias(s[1:], NORMS[s[1:]])

        @block.scalar
        def _(act):
            act.dma_start(cond[:, :], t_in["cond"]).then_inc(ld_cond, 16)
            act.dma_start(pos[:, :].rearrange("p (b t c) -> p b t c", b=B, c=3)[:, 0],
                          t_in["pos"][0].rearrange("(t p) c -> p t c", p=128)).then_inc(ld_small, 16)
            act.dma_start(pos[:, :].rearrange("p (b t c) -> p b t c", b=B, c=3)[:, 1],
                          t_in["pos"][1].rearrange("(t p) c -> p t c", p=128)).then_inc(ld_small, 16)
            act.dma_start(col[:, :], t_in["col_vecs"]).then_inc(ld_small, 16)
            act.dma_start(wqkv[0][:, :, :], t_in["wqkv0"].rearrange("p (c f) -> p c f", f=D)).then_inc(ld_qkv[0], 16)
            act.wait_ge(angles_ready, 1)
            nc.scalar.activation(sin3[:, :, :, :].rearrange("p b t c -> p (b t c)"), angle[:, :], ACT.Sin)
            nc.scalar.activation(cos3[:, :, :, :].rearrange("p b t c -> p (b t c)"), angle_c[:, :],
                                 ACT.Sin).then_inc(sines_ready, 1)
            act.wait_ge(ld_cond, 16)
            nc.scalar.activation(cond_t[:, :], cond[:, :], ACT.Tanh, scale=0.5).then_inc(cond_tanh, 1)

            def exps(tick, r):
                it = prob_tick(tick)
                if it is None:
                    return
                a, g, kt, v = it
                l, b = att(a)
                j = R * v + r
                n = N - first_query(l, kt)
                act.wait_ge(st_full, j + 1)
                if r == 0 and v >= 2:
                    act.wait_ge(pv_done, v - 1)
                nc.scalar.activation(probs[:, j % 8, 0:n], st[j % 3][:, 0:n], ACT.Exp, scale=SCALE).then_inc(exp_done, 1)

            def take_o(tick):
                it = pv_tick(tick)
                if it is None or it[2] != TT - 1:
                    return
                G = it[3] // TT
                act.wait_ge(pv_done, TT * G + TT)
                if G >= 2:
                    wait_full(act, "fold", G - 2)
                nc.scalar.activation(o_sb[:, G % 2, :], o_acc[:, :], ACT.Copy).then_inc(o_ready, 1)

            def stage(s):
                if s[0] == "max_rows":
                    G = s[1]
                    wait_full(act, *s)
                    if G >= 2:
                        act.wait_ge(max_loaded[G % 2], 16 * (G // 2))
                    nc.scalar.activation(max_rows[:, G % 2, :], bank(*s)[0:3 * R, 0:N // 2].bitcast(bf16),
                                         ACT.Copy).then_inc(free(*s), 1)
                elif s[0] == "hT":
                    l, b, w = s[1:]
                    wait_full(act, *s)
                    act.wait_ge(mod_ready, MODS[(l,)] + 1)
                    nc.scalar.activation(hT[:, :], bank(*s)[:, :], ACT.Identity, bias=mod_shift[:, l, w, b:b + 1],
                                         scale=mod_scale[:, l, w, b:b + 1]).then_inc(free(*s), 1)
                elif s[0] == "oT":
                    wait_full(act, *s)
                    nc.scalar.activation(oT[:, :], bank(*s)[:, :], ACT.Copy).then_inc(free(*s), 1)
                elif s[0] == "qk_rows":
                    for i, name in enumerate(("q_rows", "k_rows")):
                        wait_full(act, name, *s[1:])
                        nc.scalar.activation(hidden[:, i, :], bank(name, *s[1:])[:, :], ACT.Square).then_inc(sq_ready, 1)
                elif s[0] in ("q", "k"):
                    wait_full(act, *s)
                    nc.scalar.activation(parts[int(s[0] == "k")][:, 0, :], bank(*s)[:, :], ACT.Copy).then_inc(hi_ready, 1)
                elif s[0] in ("q_mid", "k_mid"):
                    i = int(s[0] == "k_mid")
                    wait_taken(act, "k" if i else "q", s[1], s[2])
                    nc.scalar.activation(parts[i][:, 1, :], rest[i], ACT.Copy).then_inc(mid_ready, 1)
                elif s[0] == "v":
                    wait_full(act, *s)
                    act.wait_ge(consts_ready, 1 + B)
                    nc.scalar.activation(vx[s[2]][:, :, 0:HD], bank(*s)[:, :].rearrange("p (c d) -> p c d", d=HD),
                                         ACT.Copy).then_inc(free(*s), 1)
                elif s[0] == "swiglu":
                    k = hid_rows(0, s[3])
                    wait_full(act, "gate_half", *s[1:])
                    nc.scalar.activation(tanh_a[0:k, :], bank("gate_half", *s[1:])[0:k, :], ACT.Tanh,
                                         scale=0.5).then_inc(tanh_ready, 1)
                elif s[0] == "up":
                    l = s[1]
                    for i in range(HID_TILES[l]):
                        c = HID_BIAS[l] + i
                        wait_full(act, *s, i)
                        nc.scalar.activation(hidden[:, i, :], bank(*s, i)[:, :],
                                             ACT.Gelu if l < 3 else ACT.Gelu_apprx_tanh,
                                             bias=col[:, c:c + 1]).then_inc(free(*s, i), 1)
                elif s[0] == "ssm":
                    wait_full(act, *s)
                    nc.scalar.activation(hidden[:, 0, :], bank(*s)[:, :], ACT.Gelu,
                                         bias=col[:, SSM_BIAS:SSM_BIAS + 1]).then_inc(free(*s), 1)

            for p in range(LAST_POINT):
                tick, q = divmod(p, Q)
                exps(tick, q)
                if q == 2:
                    take_o(tick)
                for s in PLAN.get(p, []):
                    stage(s)

        @block.vector
        def _(dve):
            steps = [0]

            def link(ins):
                steps[0] += 1
                ins.then_inc(dve_step, 1)
                dve.wait_ge(dve_step, steps[0])

            def ones_rows(b):
                nc.vector.memset(kx[b][64:96, :, :].rearrange("p h n -> p (h n)").bitcast(i32),
                                 0x3F803F80).then_inc(ones_ready, 1)

            dve.wait_ge(ld_cond, 16)
            nc.vector.tensor_copy(cond_wide[:, 0, :, :], cond[:, :].rearrange("p (b a) -> p b a", a=1).to_broadcast([128, B, 128]))
            dve.wait_ge(ld_small, 16 * 4)
            TWO_PI = (6.28125, 0.0019340515136718750, 1.25563182796e-06)
            link(nc.vector.tensor_scalar(turns[:, :], pos[:, :], 0.15915494309189535, None, ALU.mult))
            link(nc.vector.tensor_scalar(turns[:, :], turns[:, :], 12582912.0, None, ALU.add))
            link(nc.vector.tensor_scalar(turns[:, :], turns[:, :], -12582912.0, None, ALU.add))
            link(nc.vector.scalar_tensor_tensor(angle[:, :], turns[:, :], -TWO_PI[0], pos[:, :], ALU.mult, ALU.add))
            link(nc.vector.scalar_tensor_tensor(angle[:, :], turns[:, :], -TWO_PI[1], angle[:, :], ALU.mult, ALU.add))
            link(nc.vector.scalar_tensor_tensor(angle[:, :], turns[:, :], -TWO_PI[2], angle[:, :], ALU.mult, ALU.add))
            link(nc.vector.tensor_scalar(angle[:, :], angle[:, :], 3.1415925, -3.1415925, ALU.min, ALU.max))
            link(nc.vector.tensor_scalar(angle_c[:, :], angle[:, :], -1.0, None, ALU.mult))
            link(nc.vector.tensor_tensor(angle_c[:, :], angle_c[:, :], angle[:, :], ALU.max))
            nc.vector.tensor_scalar(angle_c[:, :], angle_c[:, :], -1.0, 1.5707963267948966, ALU.mult,
                                    ALU.add).then_inc(angles_ready, 1)
            ones_rows(0)
            dve.wait_ge(cond_tanh, 1)
            link(nc.vector.scalar_tensor_tensor(cond_silu[:, :], cond_t[:, :], 1.0, cond[:, :], ALU.add, ALU.mult))
            link(nc.vector.tensor_scalar(cond_silu[:, :], cond_silu[:, :], 0.5, None, ALU.mult))
            nc.vector.tensor_copy(cond_wide[:, 1, :, :], cond_silu[:, :].rearrange("p (b a) -> p b a", a=1)
                                  .to_broadcast([128, B, 128])).then_inc(cond_ready, 1)

            def spread_angles():
                dve.wait_ge(sines_ready, 1)
                last = None
                for wide, three in ((sin_w, sin3), (cos_w, cos3)):
                    for b in range(B):
                        to = wide[:, b, :, :].rearrange("p (i t) (c h) -> p i t c h", i=2, h=H)
                        for i in range(2):
                            last = nc.vector.tensor_copy(
                                to[:, i, :, :, :],
                                three[:, b, :, :].rearrange("p t (c a) -> p t c a", a=1).to_broadcast([128, TT, 3, H]))
                link(last)

            def maxima(tick, r):
                it = max_tick(tick, None)
                if it is None:
                    return
                a, g, qt, t = it
                l, b = att(a)
                i = R * t + r
                G = t // TT
                dve.wait_ge(smax_full, i + 1)
                ins = nc.vector.tensor_reduce(nmax[:, G % 2, R * qt + r:R * qt + r + 1],
                                              smax[i % 2][:, 0:max_keys(l, qt)], AX.X, ALU.max, negate=True)
                ins.then_inc(smax_free, 1)
                if qt == TT - 1 and r == R - 1:
                    dve.wait_ge(smax_free, i + 1)
                    if G >= 2:
                        wait_full(dve, "max_rows", G - 2)
                    m = nmax[:, G % 2, :]
                    rr = nrest[:, G % 2, :]
                    part = [nmax_parts[:, G % 2, :, k, :] for k in range(3)]
                    m3 = m.rearrange("p (t r) -> p t r", r=R)
                    rr3 = rr.rearrange("p (t r) -> p t r", r=R)
                    link(nc.vector.tensor_copy(part[0], m3))
                    link(nc.vector.tensor_tensor(rr3, m3, part[0], ALU.subtract))
                    link(nc.vector.tensor_copy(part[1], rr3))
                    nc.vector.tensor_tensor(part[2], rr3, part[1], ALU.subtract).then_inc(nmax_ready, 1)

            def update(u, *use):
                l, b, w = u
                wait_full(dve, *use)
                if u in BIASED:
                    dve.wait_ge(xb_ready, BIASED.index(u) + 1)
                nc.vector.tensor_tensor(x[b][:, :, :], bank(*use)[:, :].rearrange("p (t f) -> p t f", f=D),
                                        x[b][:, :, :], ALU.add).then_inc(free(*use), 1)
                wait_taken(dve, *use)
                if l < 3 or w == 0:
                    statistics(l + w, b)

            def statistics(l, b):
                for t in range(TT):
                    last = nc.vector.bn_stats(bn[:, t, :], x[b][:, t, :])
                link(last)
                for t in range(TT):
                    last = nc.vector.bn_aggr(mv[:, t, :], bn[:, t, :])
                link(last)
                if l == 0:
                    link(nc.vector.tensor_tensor(msq[:, :], mv[:, :, 0], mv[:, :, 0], ALU.mult))
                    nc.vector.scalar_tensor_tensor(ve[:, :], msq[:, :], EPS[l], mv[:, :, 1], ALU.add,
                                                   ALU.add).then_inc(var_ready, 1)
                else:
                    nc.vector.tensor_scalar(ve[:, :], mv[:, :, 1], EPS[l], None, ALU.add).then_inc(var_ready, 1)

            def stage(s):
                if s[0] == "modcol":
                    l = s[1]
                    wait_full(dve, *s)
                    m = mod[:, l, :, :, :]
                    nc.vector.tensor_tensor(
                        m.rearrange("p w c b -> p (w c) b"), bank(*s)[:, 0:8].rearrange("p (c b) -> p c b", b=B),
                        col[:, MODB0 + 4 * l:MODB0 + 4 * l + 4].rearrange("p (c a) -> p c a", a=1).to_broadcast([128, 4, B]),
                        ALU.add).then_inc(free(*s), 1)
                    wait_taken(dve, *s)
                    nw = col[:, NW0 + 2 * l:NW0 + 2 * l + 2].rearrange("p (c a) -> p c a", a=1).to_broadcast([128, 2, B])
                    nb = col[:, NB0 + 2 * l:NB0 + 2 * l + 2].rearrange("p (c a) -> p c a", a=1).to_broadcast([128, 2, B])
                    nc.vector.scalar_tensor_tensor(mod_scale[:, l, :, :], m[:, :, 1, :], 1.0, nw, ALU.add, ALU.mult)
                    link(nc.vector.scalar_tensor_tensor(mod_shift[:, l, :, :], m[:, :, 1, :], 1.0, nb, ALU.add, ALU.mult))
                    nc.vector.tensor_tensor(mod_shift[:, l, :, :], mod_shift[:, l, :, :], m[:, :, 0, :],
                                            ALU.add).then_inc(mod_ready, 1)
                elif s[0] == "gate":
                    l = s[1]
                    wait_full(dve, *s)
                    if l:
                        dve.wait_ge(gated_ready, l)
                    g0 = (GATE_ROW0 + 2 * l) * D
                    for b in range(B):
                        last = nc.vector.tensor_tensor(
                            gates[:, :, b, :], bank(*s)[:, :].rearrange("p (w b f) -> p w b f", w=2, b=B)[:, :, b, :],
                            row[:, g0:g0 + 2 * D].rearrange("p (w f) -> p w f", f=D), ALU.add)
                    last.then_inc(free(*s), 1)
                elif s[0] == "spread":
                    spread_angles()
                    ones_rows(1)
                elif s[0] == "norm":
                    l, b, w = s[1:]
                    if l == 0 and w == 0:
                        dve.wait_ge(ld_x, 32)
                        statistics(0, b)
                    n = NORMS[s[1:]]
                    dve.wait_ge(rstd_ready, n + 1)
                    if n:
                        prev = [h for h, k in HTS.items() if k == n - 1][0]
                        wait_full(dve, "hT", *prev)
                    for t in range(TT):
                        if l == 0:
                            last = nc.vector.tensor_scalar(xn[:, t, :], x[b][:, t, :], rstd[:, t:t + 1], None, ALU.mult)
                        else:
                            last = nc.vector.tensor_scalar(xn[:, t, :], x[b][:, t, :], mv[:, t, 0:1], rstd[:, t:t + 1],
                                                           ALU.subtract, ALU.mult)
                    last.then_inc(xn_ready, 1)
                elif s[0] == "qk_rows":
                    dve.wait_ge(sq_ready, 2 * (s[2] + 1))
                    sq = hidden[:, 0:2, :].rearrange("p i (t d h) -> p (i t) h d", d=HD, h=H)
                    link(nc.vector.tensor_reduce(ss[:, :].rearrange("p (c h) -> p c h", h=H), sq, AX.X, ALU.add))
                    nc.vector.tensor_scalar(ss[:, :], ss[:, :], 1.0 / HD, EPS[0], ALU.mult, ALU.add).then_inc(ss_ready, 1)
                elif s[0] == "qk_scale":
                    dve.wait_ge(qk_rs_ready, s[2] + 1)
                    last = None
                    for i, name in enumerate(("q_rows", "k_rows")):
                        rs = qk_rs[:, 64 * i:64 * i + 64].rearrange("p (t a h) -> p t a h", a=1, h=H)
                        last = nc.vector.tensor_tensor(
                            qk[:, i, :].rearrange("p (t d h) -> p t d h", d=HD, h=H),
                            bank(name, *s[1:])[:, :].rearrange("p (t d h) -> p t d h", d=HD, h=H),
                            rs.to_broadcast([128, TT, HD, H]), ALU.mult)
                        last.then_inc(free(name, *s[1:]), 1)
                    wait_taken(dve, "q_rows", *s[1:])
                    wait_taken(dve, "k_rows", *s[1:])
                    for i in range(2):
                        w = row[:, QKW0 + D * i:QKW0 + D * i + D].rearrange("p (a c) -> p a c", a=1)
                        rows = qk[:, i, :].rearrange("p (t c) -> p t c", c=D)
                        last = nc.vector.tensor_tensor(rows, rows, w.to_broadcast([128, TT, D]), ALU.mult)
                    link(last)
                elif s[0] == "rope":
                    b = s[2]
                    pairs = qk[:, :, :].rearrange("p i (t e f h) -> p (i t) e f h", e=HD // 2, f=2, h=H)
                    even, odd = pairs[:, :, 0:3, 0, :], pairs[:, :, 0:3, 1, :]
                    cw = cos_w[:, b, :, :].rearrange("p c (e h) -> p c e h", h=H)
                    sw = sin_w[:, b, :, :].rearrange("p c (e h) -> p c e h", h=H)
                    n = 2 * TT * 3 * H
                    flat = hidden[:, :, :].rearrange("p i n -> p (i n)")
                    ec, os, es, oc = [flat[:, k * n:(k + 1) * n].rearrange("p (c e h) -> p c e h", e=3, h=H) for k in range(4)]
                    nc.vector.tensor_tensor(ec, even, cw, ALU.mult)
                    nc.vector.tensor_tensor(os, odd, sw, ALU.mult)
                    nc.vector.tensor_tensor(es, even, sw, ALU.mult)
                    link(nc.vector.tensor_tensor(oc, odd, cw, ALU.mult))
                    nc.vector.tensor_tensor(even, ec, os, ALU.subtract)
                    nc.vector.tensor_tensor(odd, es, oc, ALU.add).then_inc(qk_ready, 1)
                elif s[0] in ("q", "k"):
                    i = int(s[0] == "k")
                    dve.wait_ge(hi_ready, 2 * (s[1] * B + s[2]) + i + 1)
                    nc.vector.tensor_tensor(rest[i], bank(*s)[:, :], parts[i][:, 0, :],
                                            ALU.subtract).then_inc(free(*s), 1)
                elif s[0] == "fold":
                    G = s[1]
                    a, g = divmod(G, GROUPS)
                    wait_full(dve, *s)
                    if g == 0 and a:
                        wait_full(dve, "oT", *att(a - 1))
                    if G:
                        wait_taken(dve, "fold", G - 1)
                    o = bank(*s)[:, :].rearrange("p (t r c) -> p t r c", r=R, c=VW)
                    link(nc.vector.reciprocal(rden[:, :, :], o[:, :, :, HD]))
                    nc.vector.tensor_tensor(
                        o_rows[:, :, R * HD * g:R * HD * (g + 1)].rearrange("p t (r d) -> p t r d", d=HD),
                        o[:, :, :, 0:HD], rden[:, :, :].rearrange("p t (r a) -> p t r a", a=1).to_broadcast([128, TT, R, HD]),
                        ALU.mult).then_inc(free(*s), 1)
                elif s[0] == "out":
                    update((s[1], s[2], 0), *s)
                elif s[0] == "ssm_out":
                    update((3, s[2], 0), *s)
                elif s[0] == "down" and s[3] == TT - 1:
                    update((s[1], s[2], 1), "down", s[1], s[2])
                elif s[0] == "swiglu":
                    k = hid_rows(0, s[3])
                    dve.wait_ge(tanh_ready, s[2] * HID_TILES[0] + s[3] + 1)
                    nc.vector.scalar_tensor_tensor(tanh_a[0:k, :], tanh_a[0:k, :], 1.0, bank("gate_half", *s[1:])[0:k, :],
                                                   ALU.add, ALU.mult).then_inc(free("gate_half", *s[1:]), 1)
                    wait_taken(dve, "gate_half", *s[1:])
                    wait_full(dve, "up_half", *s[1:])
                    nc.vector.scalar_tensor_tensor(hidden[0:k, s[3], :], tanh_a[0:k, :], 0.5, bank("up_half", *s[1:])[0:k, :],
                                                   ALU.mult, ALU.mult).then_inc(free("up_half", *s[1:]), 1)

            for p in range(LAST_POINT):
                tick, q = divmod(p, Q)
                maxima(tick, q)
                for s in PLAN.get(p, []):
                    stage(s)

        @block.tensor
        def _(pe):
            mm = nc.tensor.matmul

            def scores_for_max(tick, r):
                it = max_tick(tick, None)
                if it is None:
                    return
                a, g, qt, t = it
                l, b = att(a)
                i = R * t + r
                h = R * g + r
                n = max_keys(l, qt)
                if t % ATT_TICKS == 0 and r == 0:
                    pe.wait_ge(sp_terms[b], 16 * 12 * (l + 1))
                    pe.wait_ge(pool_terms[b], 16 * 6 * (l + 1))
                    if a == 0:
                        pe.wait_ge(consts_ready, 1)
                if i >= 2:
                    pe.wait_ge(smax_free, i - 1)
                last = mm(smax[i % 2][:, 0:n], qx[b][0:TERM_ROWS, h, 128 * qt:128 * qt + 128], kx[b][0:TERM_ROWS, h, 0:n],
                          start=True, stop=not CAUSAL[l])
                if CAUSAL[l]:
                    last = mm(smax[i % 2][:, n - 128:n], ident16[:, :], mask_s[:, :], start=False, stop=True)
                last.then_inc(smax_full, 1)

            def scores_turned(tick, r):
                it = prob_tick(tick)
                if it is None:
                    return
                a, g, kt, v = it
                l, b = att(a)
                j = R * v + r
                h = R * g + r
                G = v // TT
                q0 = first_query(l, kt)
                if kt == 0 and r == 0:
                    pe.wait_ge(max_loaded[G % 2], 16 * (G // 2 + 1))
                if j >= 3:
                    pe.wait_ge(exp_done, j - 2)
                last = mm(st[j % 3][:, 0:N - q0], kx[b][0:ROWS, h, 128 * kt:128 * kt + 128], qx[b][0:ROWS, h, q0:N],
                          start=True, stop=not CAUSAL[l])
                if CAUSAL[l]:
                    last = mm(st[j % 3][:, 0:128], ident16[:, :], mask_t[:, :], start=False, stop=True)
                last.then_inc(st_full, 1)

            def times_v(tick):
                it = pv_tick(tick)
                if it is None:
                    return
                a, g, kt, v = it
                l, b = att(a)
                q0 = first_query(l, kt)
                pe.wait_ge(exp_done, R * v + R)
                if kt == 0:
                    if v:
                        pe.wait_ge(o_ready, v // TT)
                    if g == 0:
                        wait_taken(pe, "v", l, b)
                for r in range(R):
                    last = mm(o_acc[VW * r:VW * r + VW, q0:N], vx[b][:, H * kt + R * g + r, :],
                              probs[:, (R * v + r) % 8, 0:N - q0], start=kt == 0, stop=kt == TT - 1)
                last.then_inc(pv_done, 1)

            def stage(s):
                if s[0] == "modcol":
                    l = s[1]
                    c = cond if l == 0 else cond_silu
                    pe.wait_ge(ld_ada[l], 16)
                    if l == 0:
                        pe.wait_ge(ld_cond, 16)
                    else:
                        pe.wait_ge(cond_ready, 1)
                    wait_free(pe, *s)
                    for k, chunk in enumerate((0, 1, 3, 4)):
                        last = mm(bank(*s)[:, B * k:B * k + B], wada[l][:, chunk, :], c[:, :], start=True, stop=True)
                    last.then_inc(full(*s), 1)
                elif s[0] == "gate":
                    l = s[1]
                    pe.wait_ge(cond_ready, 1)
                    wait_free(pe, *s)
                    for w, chunk in enumerate((2, 5)):
                        for b in range(B):
                            o = D * (B * w + b)
                            last = mm(bank(*s)[:, o:o + D], cond_wide[:, int(l > 0), b, :], wada[l][:, chunk, :],
                                      start=True, stop=True)
                    last.then_inc(full(*s), 1)
                elif s[0] == "max_rows":
                    G = s[1]
                    pe.wait_ge(nmax_ready, G + 1)
                    wait_free(pe, *s)
                    for t in range(TT):
                        last = nc.tensor.transpose(bank(*s)[0:3 * R, 64 * t:64 * t + 64].bitcast(bf16),
                                                   nmax_parts[:, G % 2, t, :, :].rearrange("p k r -> p (k r)"), ident16[:, :])
                    last.then_inc(full(*s), 1)
                elif s[0] == "fold":
                    G = s[1]
                    pe.wait_ge(o_ready, G + 1)
                    wait_free(pe, *s)
                    for t in range(TT):
                        last = nc.tensor.transpose(bank(*s)[:, 128 * t:128 * t + 128], o_sb[:, G % 2, 128 * t:128 * t + 128],
                                                   ident[:, :])
                    last.then_inc(full(*s), 1)
                elif s[0] == "oT":
                    for g in range(GROUPS):
                        wait_taken(pe, "fold", GROUPS * (s[1] * B + s[2]) + g)
                    wait_free(pe, *s)
                    for t in range(TT):
                        last = nc.tensor.transpose(bank(*s)[:, 128 * t:128 * t + 128], o_rows[:, t, :], ident[:, :])
                    last.then_inc(full(*s), 1)
                elif s[0] == "hT":
                    pe.wait_ge(xn_ready, HTS[s[1:]] + 1)
                    if HTS[s[1:]] == 0:
                        pe.wait_ge(identity_ready, 1)
                    wait_free(pe, *s)
                    for t in range(TT):
                        last = nc.tensor.transpose(bank(*s)[:, 128 * t:128 * t + 128], xn[:, t, :], ident[:, :])
                    last.then_inc(full(*s), 1)
                elif s[0] == "out":
                    l, b = s[1:]
                    wait_taken(pe, "oT", *s[1:])
                    pe.wait_ge(gated_ready, l + 1)
                    wait_free(pe, *s)
                    for t in range(TT):
                        last = mm(bank(*s)[:, D * t:D * t + D], oT[:, 128 * t:128 * t + 128], wout_g[l][b][:, :],
                                  start=True, stop=True)
                    last.then_inc(full(*s), 1)
                elif s[0] == "qk_rows":
                    l, b = s[1:]
                    wait_taken(pe, "hT", l, b, 0)
                    pe.wait_ge(ld_qkv[l], 16)
                    for i, name in enumerate(("q_rows", "k_rows")):
                        wait_free(pe, name, l, b)
                        for t in range(TT):
                            last = mm(bank(name, l, b)[:, D * t:D * t + D], hT[:, 128 * t:128 * t + 128], wqkv[l][:, i, :],
                                      start=True, stop=True)
                        last.then_inc(full(name, l, b), 1)
                elif s[0] == "v":
                    l, b = s[1:]
                    wait_taken(pe, "hT", l, b, 0)
                    pe.wait_ge(ld_qkv[l], 16)
                    wait_free(pe, *s)
                    for t in range(TT):
                        last = mm(bank(*s)[:, D * t:D * t + D], hT[:, 128 * t:128 * t + 128], wqkv[l][:, 2, :],
                                  start=True, stop=True)
                    last.then_inc(full(*s), 1)
                elif s[0] in ("q", "k"):
                    l, b = s[1:]
                    i = int(s[0] == "k")
                    wait_free(pe, *s)
                    if l == 0:
                        pe.wait_ge(qk_ready, b + 1)
                        for t in range(TT):
                            last = nc.tensor.transpose(bank(*s)[:, 128 * t:128 * t + 128], qk[:, i, 128 * t:128 * t + 128],
                                                       ident[:, :])
                    else:
                        wait_taken(pe, "hT", l, b, 0)
                        pe.wait_ge(ld_qkv[l], 16)
                        last = mm(bank(*s)[:, :], wqkv[l][:, i, :], hT[:, :], start=True, stop=True)
                    last.then_inc(full(*s), 1)
                elif s[0] == "swiglu":
                    l, b, i = s[1:]
                    k = hid_rows(0, i)
                    if i == 0:
                        wait_taken(pe, "hT", l, b, 1)
                        pe.wait_ge(ld_w[0], 16 * W_LOADS[0])
                    for w, name in enumerate(("gate_half", "up_half")):
                        wait_free(pe, name, *s[1:])
                        mm(bank(name, *s[1:])[0:k, :], wup0[:, w, 128 * i:128 * i + k], hT[:, :],
                           start=True, stop=True).then_inc(full(name, *s[1:]), 1)
                elif s[0] == "up":
                    l, b = s[1:]
                    wait_taken(pe, "hT", l, b, 1)
                    pe.wait_ge(ld_w[l], 16 * W_LOADS[l])
                    for i in range(HID_TILES[l]):
                        wait_free(pe, *s, i)
                        mm(bank(*s, i)[:, :], wup[l][:, 128 * i:128 * i + 128], hT[:, :],
                           start=True, stop=True).then_inc(full(*s, i), 1)
                elif s[0] == "ssm":
                    wait_taken(pe, "hT", 3, s[2], 0)
                    pe.wait_ge(ld_w[3], 16 * W_LOADS[3])
                    wait_free(pe, *s)
                    mm(bank(*s)[:, :], wssm[:, :], hT[:, :], start=True, stop=True).then_inc(full(*s), 1)
                elif s[0] == "ssm_out":
                    wait_taken(pe, "ssm", 3, s[2])
                    pe.wait_ge(gated_ready, 4)
                    wait_free(pe, *s)
                    for t in range(TT):
                        last = mm(bank(*s)[:, D * t:D * t + D], hidden[:, 0, 128 * t:128 * t + 128], wout_g[3][s[2]][:, :],
                                  start=True, stop=True)
                    last.then_inc(full(*s), 1)
                elif s[0] == "down":
                    l, b, t = s[1:]
                    use = ("down", l, b)
                    if t == 0:
                        for i in range(HID_TILES[l]):
                            wait_taken(pe, "up_half" if l == 0 else "up", l, b, i)
                        pe.wait_ge(gated_ready, l + 1)
                        wait_free(pe, *use)
                    for i in range(HID_TILES[l]):
                        k = hid_rows(l, i)
                        last = mm(bank(*use)[:, D * t:D * t + D], hidden[0:k, i, 128 * t:128 * t + 128],
                                  wdown_g[l][b][0:k, i, :], start=i == 0, stop=i == HID_TILES[l] - 1)
                    if t == TT - 1:
                        last.then_inc(full(*use), 1)

            for p in range(LAST_POINT):
                tick, q = divmod(p, Q)
                scores_for_max(tick, q)
                scores_turned(tick, q)
                if q == 1:
                    times_v(tick)
                for s in PLAN.get(p, []):
                    stage(s)


def kernel(**inputs):
    import numpy as np
    import concourse.bacc as bacc
    from concourse.bass_utils import run_bass_kernel_spmd

    v = {k: np.asarray(a) for k, a in inputs.items()}
    f = np.ascontiguousarray
    turned = np.arange(D).reshape(H, HD).T.reshape(D)
    shared = np.repeat(np.arange(D // R).reshape(GROUPS, 1, HD), R, axis=1).reshape(D)

    qkv0, qkv1 = v["L0_cond_qkv_w"].T, v["L1_cond_Wqkv"]
    wq2, wk2, wv2 = v["L2_cond_wq"].T, v["L2_cond_wk"].T, v["L2_cond_wv"].T
    ada_b = [v["L0_cond_ada_b"], v["L1_cond_bada"], v["L2_cond_bc"], v["L3_cond_ada_b"]]
    one, zero = np.ones(D, np.float32), np.zeros(D, np.float32)
    norm_w = [v["L0_cond_norm1_w"], v["L0_cond_norm2_w"], v["L1_cond_g1"], v["L1_cond_g2"], one, one, one, one]
    norm_b = [zero, zero, v["L1_cond_be1"], v["L1_cond_be2"], zero, zero, zero, zero]
    cols = [b.reshape(6, D)[c] for b in ada_b for c in (0, 1, 3, 4)] + norm_w + norm_b
    cols += [*v["L1_cond_b1"].reshape(4, D), *v["L2_cond_b1"].reshape(4, D), v["L3_cond_ssm_b1"],
             *v["L3_cond_ff_b1"].reshape(2, D)]
    rows = [v["L0_cond_proj_b"], v["L1_cond_bproj"], v["L1_cond_b2"], v["L2_cond_b2"], v["L3_cond_ssm_b2"],
            v["L3_cond_ff_b2"]]
    rows += [b.reshape(6, D)[c] for b in ada_b for c in (2, 5)]
    rows += [np.repeat(v["L0_cond_q_norm_w"], H), np.repeat(v["L0_cond_k_norm_w"], H)]
    arrays = {
        "x": f(v["x"]), "cond": f(v["cond_1024"].T), "pos": f(v["fside_BxSx3_0"]),
        "col_vecs": f(np.stack(cols, axis=1)), "row_vecs": f(np.concatenate(rows)),
        "wqkv0": f(np.concatenate([qkv0[:, :D][:, turned], qkv0[:, D:2 * D][:, turned], qkv0[:, 2 * D:]], axis=1)),
        "wqkv1": f(np.concatenate([qkv1[:, :D][:, turned], qkv1[:, D:2 * D][:, turned], qkv1[:, 2 * D:]], axis=1)),
        "wqkv2": f(np.concatenate([wq2[:, turned], wk2[:, shared][:, turned], wv2[:, shared]], axis=1)),
        "wout0": f(v["L0_cond_proj_w"].T), "wout1": f(v["L1_cond_Wproj"]), "wout2": f(v["L2_cond_wo"].T),
        "wout3": f(v["L3_cond_ssm_w2"]), "wssm": f(v["L3_cond_ssm_w1"]),
        "wup0": f(np.concatenate([v["L0_cond_w1"].T, v["L0_cond_w3"].T], axis=1)), "wup1": f(v["L1_cond_W1"]),
        "wup2": f(v["L2_cond_w1"].T), "wup3": f(v["L3_cond_ff_w1"]),
        "wdown0": f(v["L0_cond_w2"].T), "wdown1": f(v["L1_cond_W2"]), "wdown2": f(v["L2_cond_w2"].T),
        "wdown3": f(v["L3_cond_ff_w2"]),
        "wada0": f(v["L0_cond_ada_w"].T), "wada1": f(v["L1_cond_Wada"]), "wada2": f(v["L2_cond_wc"].T),
        "wada3": f(v["L3_cond_ada_w"]),
    }
    nc = bacc.Bacc("TRN2", target_bir_lowering=False, num_devices=1)
    t_in = {k: nc.dram_tensor(f"in_{k}", a.shape, mybir.dt.float32, kind="ExternalInput").ap() for k, a in arrays.items()}
    out = nc.dram_tensor("out", (B, N, D), mybir.dt.float32, kind="ExternalOutput").ap()
    program(nc, t_in, out)
    r = run_bass_kernel_spmd(nc, [{f"in_{k}": a for k, a in arrays.items()}], core_ids=[0])
    return r.results[0]["out"]
```

```python
from contextlib import ExitStack

import concourse.bass as bass
from concourse import mybir

B, N, D = 2, 512, 128
LAYERS = 4
ATT_LAYERS = 3
H, HD = 16, 8
R = 4
GROUPS = H // R
TT = N // 128
TERMS = 9
NEWTON_STEPS = 3
TERM_ROWS = TERMS * HD
MAX_ROWS = 3
ROWS = TERM_ROWS + MAX_ROWS
VW = 32
SCALE = float(HD) ** -0.5
NEG = -1e30
HID0 = 341
HID_TILES = [3, 4, 4, 2]
EPS = [1e-6, 1e-5, 1e-5, 1e-6]
CAUSAL = [False, True, False]
BIAS_ROWS = {(0, 0): 0, (1, 0): 1, (1, 1): 2, (2, 1): 3, (3, 0): 4, (3, 1): 5}
GATE_ROW0 = len(BIAS_ROWS)
QKW0 = (GATE_ROW0 + 2 * LAYERS) * D
ROW_VECS = QKW0 + 2 * D
MODB0, NW0, NB0, HB0 = 0, 16, 24, 32
HID_BIAS = {1: HB0, 2: HB0 + 4, 3: HB0 + 9}
SSM_BIAS = HB0 + 8
COL_VECS = HB0 + 11

MAX_BANKS = 3
ST_BANKS = 2
SPARES = 2
PV_MIDDLE = ((0,), (1,), (2,), (3,))
PV_LAST = ((0, 1), (2, 3), (), ())
PV_FIRST = ((), (), (0, 1), (2, 3))
NORM_GAP = 2
HT_GAP = 2
ROPE_POINT = 0
PARTS_GAP = 3
LAG = 6
LEAD = 5
ATT_TICKS = GROUPS * TT
N_ATT = ATT_LAYERS * B
TICKS = N_ATT * ATT_TICKS
Q = 4


def make_plan():
    plan = {}

    def put(point, *stage):
        plan.setdefault(point, []).append(stage)
        if stage[0] == "norm" and (stage[1], stage[3]) in BIAS_ROWS:
            if stage[1]:
                put(point, "bias", *stage[1:])
        return point

    def parts(p, l, b):
        put(p, "q", l, b)
        put(p + 1, "k", l, b)
        put(p, "q_terms", l, b, 0)
        put(p + 1, "q_mid", l, b)
        p = put(p + 2, "k_mid", l, b)
        for i in range(1, 3):
            put(p + 3 * i - 1, "q_terms", l, b, i)
        put(p + 8, "k_low_terms", l, b)
        if l:
            p = put(p + 3, "v", l, b)
        return p

    def mlp(p, l, b, gap):
        if l == 0:
            for i in range(HID_TILES[0]):
                p = put(p + 1, "swiglu", l, b, i)
        else:
            p = put(p + gap, "up", l, b)
        for tt in range(TT):
            p = put(p + 1, "down", l, b, tt)
        return p

    def last_block(p, b):
        p = put(p + 2, "norm", 3, b, 0)
        p = put(p + 2, "hT", 3, b, 0)
        p = put(p + 2, "ssm", 3, b)
        p = put(p + 2, "ssm_out", 3, b)
        p = put(p + 2, "norm", 3, b, 1)
        p = put(p + 2, "hT", 3, b, 1)
        p = mlp(p, 3, b, 2)
        put(p, "store", b)

    put(0, "stats", 0)
    put(0, "norm", 0, 0, 0)
    put(1, "modcol", 0)
    put(1, "hT", 0, 0, 0)
    put(2, "stats", 1)
    put(2, "angles")
    put(2, "norm", 0, 1, 0)
    put(2, "spread")
    put(3, "qk_rows", 0, 0)
    put(4, "v", 0, 0)
    put(4, "hT", 0, 1, 0)
    put(5, "qk_rows", 0, 1)
    put(5, "v", 0, 1)
    put(6, "qk_scale", 0, 0)
    put(6, "rope", 0, 0)
    parts(7, 0, 0)
    put(9, "qk_scale", 0, 1)
    base = Q * LEAD
    put(base + ROPE_POINT, "rope", 0, 1)
    parts(base + PARTS_GAP, 0, 1)
    put(base + 3, "condition")
    put(base + 22, "gate", 0)
    for b in range(B):
        put(base + 23, "bias", 0, b, 0)
    for l in range(1, LAYERS):
        put(base + 13 + 14 * l, "modcol", l)
        put(base + 15 + 14 * l, "gate", l)
    for a in range(N_ATT):
        l, b = divmod(a, B)
        for g in range(GROUPS):
            G = a * GROUPS + g
            put(base + Q * (4 * G + 4) + 2, "max_rows", G)
            p = put(base + Q * (4 * G + LAG + 5), "fold", G)
        p = put(p + 3, "oT", l, b)
        p = put(p + 1, "out", l, b)
        p = put(p + NORM_GAP, "norm", l, b, 1)
        p = put(p + HT_GAP, "hT", l, b, 1)
        p = mlp(p, l, b, 2)
        if l + 1 < ATT_LAYERS:
            p = put(p + NORM_GAP, "norm", l + 1, b, 0)
            p = put(p + HT_GAP, "hT", l + 1, b, 0)
            parts(p + 1, l + 1, b)
        else:
            last_block(p, b)
    return plan


PLAN = make_plan()
LAST_POINT = max(max(PLAN), Q * (LEAD + TICKS + LAG + 1)) + 1


def stages(name=None):
    out = [s for p in sorted(PLAN) for s in PLAN[p]]
    return [s[1:] for s in out if s[0] == name] if name else out


def spare_uses():
    out = []
    for s in stages():
        if s[0] in ("modcol", "gate", "fold", "max_rows", "hT", "oT", "v", "q", "k", "ssm"):
            out.append(s)
        elif s[0] == "qk_rows":
            out += [("q_rows", *s[1:]), ("k_rows", *s[1:])]
        elif s[0] == "swiglu":
            out += [("gate_half", *s[1:]), ("up_half", *s[1:])]
        elif s[0] == "up":
            out += [("up", *s[1:], i) for i in range(HID_TILES[s[1]])]
        elif s[0] in ("out", "ssm_out"):
            out += [(*s, 0), (*s, 1)]
        elif s[0] == "down" and s[3] % 2 == 0:
            out.append(("down", *s[1:3], s[3] // 2))
    return out


SPARE = {s: n for n, s in enumerate(spare_uses())}
assert len(SPARE) == len(spare_uses())


def order(name):
    return {s: n for n, s in enumerate(stages(name))}


NORMS = order("norm")
HTS = order("hT")
MODS = order("modcol")
BIASED = stages("bias")


def hid_rows(l, i):
    return min(128, HID0 - 128 * i) if l == 0 else 128


def program(nc, t_in, out):
    f32, bf16, i32 = mybir.dt.float32, mybir.dt.bfloat16, mybir.dt.int32
    ALU, ACT, AX = mybir.AluOpType, mybir.ActivationFunctionType, mybir.AxisListType
    ctx = ExitStack()
    with ctx:
        def sb(name, shape, dt=f32):
            return ctx.enter_context(nc.sbuf_tensor(name, shape, dt))

        def sem(name):
            return ctx.enter_context(nc.semaphore(name))

        wqkv = [sb(f"wqkv{l}", [128, 3, D]) for l in range(ATT_LAYERS)]
        wout = [sb(f"wout{l}", [128, D]) for l in range(LAYERS)]
        wada = [sb(f"wada{l}", [128, 6, D]) for l in range(LAYERS)]
        wup0 = sb("wup0", [128, 2, HID0])
        wup = [None] + [sb(f"wup{l}", [128, HID_TILES[l] * 128]) for l in range(1, LAYERS)]
        wssm = sb("wssm", [128, D])
        wdown = [sb(f"wdown{l}", [128, HID_TILES[l], D]) for l in range(LAYERS)]
        wout_g = [[sb(f"wout_g{l}", [128, D]), wout[l]] for l in range(LAYERS)]
        wdown_g = [[sb(f"wdown_g{l}", [128, HID_TILES[l], D]), wdown[l]] for l in range(LAYERS)]
        bias_g = {k: sb(f"bias_g{k[0]}{k[1]}", [128, B, D]) for k in BIAS_ROWS}
        col = sb("col", [128, COL_VECS])
        row = sb("row", [128, ROW_VECS])
        cond = sb("cond", [128, B])
        cond_t = sb("cond_t", [128, B])
        cond_silu = sb("cond_silu", [128, B])
        cond_wide = sb("cond_wide", [128, 2, B, 128])
        mod = sb("mod", [128, LAYERS, 2, 2, B])
        mod_scale = sb("mod_scale", [128, LAYERS, 2, B])
        mod_shift = sb("mod_shift", [128, LAYERS, 2, B])
        gates = sb("gates", [128, 2, B, D])
        pos = sb("pos", [128, B * TT * 3])
        turns = sb("turns", [128, B * TT * 3])
        angle = sb("angle", [128, B * TT * 3])
        angle_c = sb("angle_c", [128, B * TT * 3])
        sin3 = sb("sin3", [128, B, TT, 3])
        cos3 = sb("cos3", [128, B, TT, 3])
        sin_w = sb("sin_w", [128, B, 2 * TT, 3 * H])
        cos_w = sb("cos_w", [128, B, 2 * TT, 3 * H])
        ident = sb("ident", [128, 128])
        ident16 = sb("ident16", [128, 128], bf16)
        mask_s = sb("mask_s", [128, 128], bf16)
        mask_t = sb("mask_t", [128, 128], bf16)
        ones3 = sb("ones3", [MAX_ROWS, N], bf16)
        minus_half = sb("minus_half", [128, TT])
        sine_made_first = sb("sine_made_first", [128, TT])
        x = [sb(f"x{b}", [128, TT, D]) for b in range(B)]
        bn = sb("bn", [128, TT, 6])
        mv = sb("mv", [128, TT, 2])
        msq = sb("msq", [128, TT])
        ve = sb("ve", [128, TT])
        rstd = sb("rstd", [128, TT])
        xn = sb("xn", [128, TT, D])
        hT = sb("hT", [128, N])
        hidden = sb("hidden", [128, 4, N])
        tanh_a = sb("tanh_a", [128, N])
        probs = sb("probs", [128, 8, N])
        qk = sb("qk", [128, 2, N])
        ss = sb("ss", [128, 2 * TT * H])
        qk_rs = sb("qk_rs", [128, 2 * TT * H])
        newton = sb("newton", [128, 2 * TT * H])
        rows_of = [qk[:, :, :], probs[:, 0:2, :]]
        squares_of = [hidden[:, 0:2, :], probs[:, 4:6, :]]
        parts = [sb(f"{n}_parts", [128, 3, N], bf16) for n in "qk"]
        rest = [qk[:, 0, :], qk[:, 1, :]]
        qx = [sb(f"qx{b}", [128, H, N], bf16) for b in range(B)]
        kx = [sb(f"kx{b}", [128, H, N], bf16) for b in range(B)]
        vx = [sb(f"vx{b}", [128, TT * H, VW]) for b in range(B)]
        nmax = sb("nmax", [128, 2, TT * R])
        nrest = sb("nrest", [128, 2, TT * R])
        nmax_parts = sb("nmax_parts", [128, 2, TT, 3, R], bf16)
        max_rows = sb("max_rows", [3 * R, 2, N], bf16)
        o_sb = sb("o_sb", [128, 2, N])
        rden = sb("rden", [128, TT, R])
        o_rows = sb("o_rows", [128, TT, D])
        oT = sb("oT", [128, N])

        smax = [ctx.enter_context(nc.psum_tensor(f"smax{i}", [128, N], f32)) for i in range(MAX_BANKS)]
        st = [ctx.enter_context(nc.psum_tensor(f"st{i}", [128, N], f32)) for i in range(ST_BANKS)]
        o_acc = ctx.enter_context(nc.psum_tensor("o_acc", [128, N], f32))
        spare = [ctx.enter_context(nc.psum_tensor(f"spare{i}", [128, N], f32)) for i in range(SPARES)]

        ld_x = [sem(f"ld_x{b}") for b in range(B)]
        ld_cond = sem("ld_cond")
        ld_small = sem("ld_small")
        ld_ada = [sem(f"ld_ada{l}") for l in range(LAYERS)]
        ld_qkv = [sem(f"ld_qkv{l}") for l in range(ATT_LAYERS)]
        ld_w = [sem(f"ld_w{l}") for l in range(LAYERS)]
        identity_ready = sem("identity_ready")
        consts_ready = sem("consts_ready")
        ones_ready = sem("ones_ready")
        ones_laid = sem("ones_laid")
        pool_step = sem("pool_step")
        dve_step = sem("dve_step")
        act_step = sem("act_step")
        cond_tanh = sem("cond_tanh")
        cond_ready = sem("cond_ready")
        mod_ready = sem("mod_ready")
        gated_ready = sem("gated_ready")
        angles_ready = sem("angles_ready")
        sines_ready = sem("sines_ready")
        spare_full = [sem(f"spare_full{i}") for i in range(SPARES)]
        spare_free = [sem(f"spare_free{i}") for i in range(SPARES)]
        xb_ready = sem("xb_ready")
        var_ready = sem("var_ready")
        rstd_ready = sem("rstd_ready")
        xn_ready = sem("xn_ready")
        tanh_ready = sem("tanh_ready")
        qk_ready = sem("qk_ready")
        hi_ready = sem("hi_ready")
        mid_ready = sem("mid_ready")
        lo_ready = sem("lo_ready")
        sp_terms = [sem(f"sp_terms{b}") for b in range(B)]
        pool_terms = [sem(f"pool_terms{b}") for b in range(B)]
        smax_full = sem("smax_full")
        smax_free = sem("smax_free")
        nmax_ready = sem("nmax_ready")
        max_loaded = [sem(f"max_loaded{i}") for i in range(2)]
        st_full = sem("st_full")
        exp_done = sem("exp_done")
        pv_done = sem("pv_done")
        o_ready = sem("o_ready")
        stored = sem("stored")

        W_LOADS = [4, 3, 3, 4]

        def bank(*use):
            return spare[SPARE[use] % SPARES]

        def wait_full(eng, *use):
            n = SPARE[use]
            eng.wait_ge(spare_full[n % SPARES], n // SPARES + 1)

        def full(*use):
            return spare_full[SPARE[use] % SPARES]

        def free(*use):
            return spare_free[SPARE[use] % SPARES]

        def wait_taken(eng, *use):
            n = SPARE[use]
            eng.wait_ge(spare_free[n % SPARES], n // SPARES + 1)

        def wait_free(pe, *use):
            n = SPARE[use]
            if n >= SPARES:
                pe.wait_ge(spare_free[n % SPARES], n // SPARES)

        def att(a):
            l, b = divmod(a, B)
            return l, b

        def max_keys(l, qt):
            return 128 * (qt + 1) if CAUSAL[l] else N

        def first_query(l, kt):
            return 128 * kt if CAUSAL[l] else 0

        def max_tick(tick, T):
            t = tick - LEAD
            return (t // ATT_TICKS, t // TT % GROUPS, t % TT, t) if 0 <= t < TICKS else None

        def prob_tick(tick):
            return max_tick(tick - LAG, None)

        def pv_tick(tick):
            return max_tick(tick - LAG - 1, None)

        def pv_heads(kt, q):
            return (PV_FIRST if kt == 0 else PV_LAST if kt == TT - 1 else PV_MIDDLE)[q]

        block = ctx.enter_context(nc.Block())

        @block.sync
        def _(sp):
            sp.dma_start(x[0][:, :, :], t_in["x"][0].rearrange("(t p) f -> p t f", p=128)).then_inc(ld_x[0], 16)
            sp.dma_start(wada[0][:, :, :], t_in["wada0"].rearrange("p (c f) -> p c f", f=D)).then_inc(ld_ada[0], 16)
            sp.dma_start(row[:, :], bass.AP(tensor=t_in["row_vecs"].tensor, offset=0,
                                               ap=[[0, 128], [1, ROW_VECS]])).then_inc(ld_small, 16)
            sp.dma_start(x[1][:, :, :], t_in["x"][1].rearrange("(t p) f -> p t f", p=128)).then_inc(ld_x[1], 16)
            sp.dma_start(wout[0][:, :], t_in["wout0"]).then_inc(ld_w[0], 16)
            sp.dma_start(wup0[:, :, :], t_in["wup0"].rearrange("p (c f) -> p c f", f=HID0)).then_inc(ld_w[0], 16)
            sp.dma_start(wdown[0][:, 0:2, :], t_in["wdown0"][0:256, :].rearrange("(t p) f -> p t f", p=128)).then_inc(ld_w[0], 16)
            sp.dma_start(wdown[0][0:HID0 - 256, 2, :], t_in["wdown0"][256:HID0, :]).then_inc(ld_w[0], 16)

            sp.wait_ge(ones_ready, 1)
            for b in range(B):
                sp.dma_start(kx[b][TERM_ROWS:ROWS, :, :],
                             ones3[:, :].rearrange("p (a n) -> p a n", a=1).to_broadcast([MAX_ROWS, H, N])).then_inc(ones_laid, 16)

            def load_layer(l):
                sp.dma_start(wada[l][:, :, :], t_in[f"wada{l}"].rearrange("p (c f) -> p c f", f=D)).then_inc(ld_ada[l], 16)
                if l < ATT_LAYERS:
                    sp.dma_start(wqkv[l][:, :, :], t_in[f"wqkv{l}"].rearrange("p (c f) -> p c f", f=D)).then_inc(ld_qkv[l], 16)
                else:
                    sp.dma_start(wssm[:, :], t_in["wssm"]).then_inc(ld_w[l], 16)
                sp.dma_start(wout[l][:, :], t_in[f"wout{l}"]).then_inc(ld_w[l], 16)
                sp.dma_start(wup[l][:, :], t_in[f"wup{l}"]).then_inc(ld_w[l], 16)
                sp.dma_start(wdown[l][:, :, :], t_in[f"wdown{l}"].rearrange("(t p) f -> p t f", p=128)).then_inc(ld_w[l], 16)

            def max_rows_out(G):
                a, g = divmod(G, GROUPS)
                wait_taken(sp, "max_rows", G)
                sp.dma_start(qx[att(a)[1]][TERM_ROWS:ROWS, R * g:R * g + R, :],
                             max_rows[:, G % 2, :]).then_inc(max_loaded[G % 2], 16)

            def q_terms(l, b, i):
                sp.wait_ge((hi_ready, mid_ready, lo_ready)[i], 2 * (l * B + b) + 1)
                for j in range(3):
                    r0 = HD * (3 * i + j)
                    sp.dma_start(qx[b][r0:r0 + HD, :, :], parts[0][:, i, :]).then_inc(sp_terms[b], 16)

            def k_low_terms(l, b):
                sp.wait_ge(lo_ready, 2 * (l * B + b) + 2)
                for i in range(3):
                    r0 = HD * (3 * i + 2)
                    sp.dma_start(kx[b][r0:r0 + HD, :, :], parts[1][:, 2, :]).then_inc(sp_terms[b], 16)

            loads = {Q * LEAD + 12 * (l + 1): l + 1 for l in range(3)}
            for p in range(LAST_POINT):
                if p in loads:
                    load_layer(loads[p])
                for s in PLAN.get(p, []):
                    if s[0] == "max_rows":
                        max_rows_out(s[1])
                    elif s[0] == "q_terms":
                        q_terms(*s[1:])
                    elif s[0] == "k_low_terms":
                        k_low_terms(*s[1:])
                    elif s[0] == "store":
                        b = s[1]
                        wait_taken(sp, "down", 3, b, 1)
                        sp.dma_start(out[b].rearrange("(t p) f -> p t f", p=128), x[b][:, :, :]).then_inc(stored, 16)
            sp.wait_ge(stored, 16 * B)

        @block.gpsimd
        def _(pool):
            pool.memset(minus_half[:, :], -0.5).then_inc(pool_step, 1)
            pool.memset(ident[:, :], 0.0)
            pool.memset(ident16[:, :], 0.0)
            pool.memset(mask_s[:, :], 0.0)
            pool.memset(mask_t[:, :], 0.0).then_inc(pool_step, 1)
            pool.wait_ge(pool_step, 2)
            pool.affine_select(out=ident[:, :], in_=ident[:, :], compare_op=ALU.not_equal, fill=1.0,
                               base=0, pattern=[[-1, 128]], channel_multiplier=1).then_inc(identity_ready, 1)
            pool.affine_select(out=ident16[:, :], in_=ident16[:, :], compare_op=ALU.not_equal, fill=1.0,
                               base=0, pattern=[[-1, 128]], channel_multiplier=1)
            pool.affine_select(out=mask_s[:, :], in_=mask_s[:, :], compare_op=ALU.is_ge, fill=NEG,
                               base=0, pattern=[[-1, 128]], channel_multiplier=1)
            pool.affine_select(out=mask_t[:, :], in_=mask_t[:, :], compare_op=ALU.is_ge, fill=NEG,
                               base=0, pattern=[[1, 128]], channel_multiplier=-1).then_inc(consts_ready, 1)
            def around_v():
                for b in range(B):
                    pool.memset(vx[b][:, :, :], 0.0).then_inc(pool_step, 1)
                    pool.wait_ge(pool_step, 3 + b)
                    pool.memset(vx[b][:, :, HD:HD + 1], 1.0).then_inc(consts_ready, 1)

            def gated(l):
                wait_taken(pool, "gate", l)
                pool.wait_ge(ld_w[l], 16 * W_LOADS[l])
                if l == 0:
                    pool.wait_ge(ld_small, 16 * 4)
                last = None
                for b in range(B):
                    pool.tensor_tensor(wout_g[l][b][:, :], wout[l][:, :], gates[:, 0, b, :], ALU.mult)
                    for i in range(HID_TILES[l]):
                        k = hid_rows(l, i)
                        last = pool.tensor_tensor(wdown_g[l][b][0:k, i, :], wdown[l][0:k, i, :],
                                                  gates[0:k, 1, b, :], ALU.mult)
                for w in range(2):
                    if (l, w) in BIAS_ROWS:
                        r = BIAS_ROWS[(l, w)] * D
                        for b in range(B):
                            last = pool.tensor_tensor(bias_g[(l, w)][:, b, :], row[:, r:r + D], gates[:, w, b, :], ALU.mult)
                last.then_inc(gated_ready, 1)

            def add_bias(u, n):
                l, b, w = u
                pool.wait_ge(gated_ready, l + 1)
                pool.wait_ge(xn_ready, TT * (n + 1))
                pool.tensor_tensor(x[b][:, :, :], x[b][:, :, :],
                                   bias_g[(l, w)][:, b:b + 1, :].to_broadcast([128, TT, D]), ALU.add).then_inc(xb_ready, 1)

            def k_terms(l, b, j):
                pool.wait_ge((hi_ready, mid_ready)[j], 2 * (l * B + b) + 2)
                for i in range(3):
                    r0 = HD * (3 * i + j)
                    pool.dma_start(kx[b][r0:r0 + HD, :, :], parts[1][:, j, :]).then_inc(pool_terms[b], 16)

            for p in range(LAST_POINT):
                for s in PLAN.get(p, []):
                    if s == ("angles",):
                        around_v()
                    elif s[0] == "norm":
                        pool.wait_ge(var_ready, NORMS[s[1:]] + 1)
                        pool.tensor_tensor(rstd[:, :], ve[:, :], minus_half[:, :], ALU.pow).then_inc(rstd_ready, 1)
                    elif s[0] == "gate":
                        gated(s[1])
                    elif s[0] in ("q_mid", "k_mid"):
                        i = int(s[0] == "k_mid")
                        n = 2 * (s[1] * B + s[2]) + i
                        if n >= 2:
                            pool.wait_ge(mid_ready, n + 1)
                            pool.tensor_tensor(parts[i][:, 2, :], rest[i], parts[i][:, 1, :],
                                               ALU.subtract).then_inc(lo_ready, 1)
                    if s[0] in ("k", "k_mid"):
                        k_terms(s[1], s[2], int(s[0] == "k_mid"))
                    elif s[0] == "bias":
                        add_bias(s[1:], NORMS[s[1:]])

        @block.scalar
        def _(act):
            act.dma_start(cond[:, :], t_in["cond"]).then_inc(ld_cond, 16)
            act.dma_start(pos[:, :].rearrange("p (b t c) -> p b t c", b=B, c=3)[:, 0],
                          t_in["pos"][0].rearrange("(t p) c -> p t c", p=128)).then_inc(ld_small, 16)
            act.dma_start(pos[:, :].rearrange("p (b t c) -> p b t c", b=B, c=3)[:, 1],
                          t_in["pos"][1].rearrange("(t p) c -> p t c", p=128)).then_inc(ld_small, 16)
            act.dma_start(col[:, :], t_in["col_vecs"]).then_inc(ld_small, 16)
            act.dma_start(wqkv[0][:, :, :], t_in["wqkv0"].rearrange("p (c f) -> p c f", f=D)).then_inc(ld_qkv[0], 16)
            act.wait_ge(pool_step, 1)
            nc.scalar.activation(sine_made_first[:, :], minus_half[:, :], ACT.Sin)

            def exps(tick, r):
                it = prob_tick(tick)
                if it is None:
                    return
                a, g, kt, v = it
                l, b = att(a)
                j = R * v + r
                n = N - first_query(l, kt)
                act.wait_ge(st_full, j + 1)
                if r == 0 and v >= 2:
                    act.wait_ge(pv_done, v - 1)
                nc.scalar.activation(probs[:, j % 8, 0:n], st[j % ST_BANKS][:, 0:n], ACT.Exp, scale=SCALE).then_inc(exp_done, 1)

            def take_o(tick):
                it = pv_tick(tick)
                if it is None or it[2] != TT - 1:
                    return
                G = it[3] // TT
                act.wait_ge(pv_done, TT * G + TT)
                if G >= 2:
                    wait_full(act, "fold", G - 2)
                nc.scalar.activation(o_sb[:, G % 2, :], o_acc[:, :], ACT.Copy).then_inc(o_ready, 1)

            def stage(s):
                if s[0] == "max_rows":
                    G = s[1]
                    wait_full(act, *s)
                    if G >= 2:
                        act.wait_ge(max_loaded[G % 2], 16 * (G // 2))
                    nc.scalar.activation(max_rows[:, G % 2, :], bank(*s)[0:3 * R, 0:N // 2].bitcast(bf16),
                                         ACT.Copy).then_inc(free(*s), 1)
                elif s[0] == "spread":
                    act.wait_ge(angles_ready, 1)
                    nc.scalar.activation(sin3[:, :, :, :].rearrange("p b t c -> p (b t c)"), angle[:, :], ACT.Sin)
                    nc.scalar.activation(cos3[:, :, :, :].rearrange("p b t c -> p (b t c)"), angle_c[:, :],
                                         ACT.Sin).then_inc(sines_ready, 1)
                elif s[0] == "condition":
                    act.wait_ge(ld_cond, 16)
                    nc.scalar.activation(cond_t[:, :], cond[:, :], ACT.Tanh, scale=0.5).then_inc(cond_tanh, 1)
                elif s[0] == "hT":
                    l, b, w = s[1:]
                    wait_full(act, *s)
                    act.wait_ge(mod_ready, MODS[(l,)] + 1)
                    nc.scalar.activation(hT[:, :], bank(*s)[:, :], ACT.Identity, bias=mod_shift[:, l, w, b:b + 1],
                                         scale=mod_scale[:, l, w, b:b + 1]).then_inc(free(*s), 1)
                elif s[0] == "oT":
                    wait_full(act, *s)
                    nc.scalar.activation(oT[:, :], bank(*s)[:, :], ACT.Copy).then_inc(free(*s), 1)
                elif s[0] == "qk_rows":
                    for i, name in enumerate(("q_rows", "k_rows")):
                        wait_full(act, name, *s[1:])
                        nc.scalar.activation(squares_of[s[2]][:, i, :], bank(name, *s[1:])[:, :], ACT.Square)
                        nc.scalar.activation(rows_of[s[2]][:, i, :], bank(name, *s[1:])[:, :],
                                             ACT.Copy).then_inc(free(name, *s[1:]), 1)
                elif s[0] in ("q", "k"):
                    wait_full(act, *s)
                    a = s[1] * B + s[2]
                    if a and s[0] == "q":
                        lb, bb = att(a - 1)
                        act.wait_ge(sp_terms[bb], 16 * 12 * (lb + 1))
                        act.wait_ge(pool_terms[bb], 16 * 6 * (lb + 1))
                    nc.scalar.activation(parts[int(s[0] == "k")][:, 0, :], bank(*s)[:, :], ACT.Copy).then_inc(hi_ready, 1)
                elif s[0] in ("q_mid", "k_mid"):
                    i = int(s[0] == "k_mid")
                    wait_taken(act, "k" if i else "q", s[1], s[2])
                    nc.scalar.activation(parts[i][:, 1, :], rest[i], ACT.Copy).then_inc(mid_ready, 1)
                elif s[0] == "v":
                    wait_full(act, *s)
                    act.wait_ge(consts_ready, 1 + B)
                    nc.scalar.activation(vx[s[2]][:, :, 0:HD], bank(*s)[:, :].rearrange("p (c d) -> p c d", d=HD),
                                         ACT.Copy).then_inc(free(*s), 1)
                elif s[0] == "swiglu":
                    k = hid_rows(0, s[3])
                    n = s[2] * HID_TILES[0] + s[3]
                    if n:
                        bb, i = divmod(n - 1, HID_TILES[0])
                        wait_taken(act, "up_half", 0, bb, i)
                    wait_full(act, "gate_half", *s[1:])
                    nc.scalar.activation(tanh_a[0:k, :], bank("gate_half", *s[1:])[0:k, :], ACT.Tanh,
                                         scale=0.5).then_inc(tanh_ready, 1)
                elif s[0] == "up":
                    l = s[1]
                    for i in range(HID_TILES[l]):
                        c = HID_BIAS[l] + i
                        wait_full(act, *s, i)
                        nc.scalar.activation(hidden[:, i, :], bank(*s, i)[:, :],
                                             ACT.Gelu if l < 3 else ACT.Gelu_apprx_tanh,
                                             bias=col[:, c:c + 1]).then_inc(free(*s, i), 1)
                elif s[0] == "ssm":
                    wait_full(act, *s)
                    nc.scalar.activation(hidden[:, 0, :], bank(*s)[:, :], ACT.Gelu,
                                         bias=col[:, SSM_BIAS:SSM_BIAS + 1]).then_inc(free(*s), 1)

            for p in range(LAST_POINT):
                tick, q = divmod(p, Q)
                exps(tick, q)
                if q == 2:
                    take_o(tick)
                for s in PLAN.get(p, []):
                    stage(s)

        @block.vector
        def _(dve):
            steps = [0]

            def link(ins):
                steps[0] += 1
                ins.then_inc(dve_step, 1)
                dve.wait_ge(dve_step, steps[0])

            nc.vector.memset(ones3[:, :], 1.0).then_inc(ones_ready, 1)

            def angles():
                dve.wait_ge(ld_small, 16 * 4)
                TWO_PI = (6.28125, 0.0019340515136718750, 1.25563182796e-06)
                link(nc.vector.tensor_scalar(turns[:, :], pos[:, :], 0.15915494309189535, None, ALU.mult))
                link(nc.vector.tensor_scalar(turns[:, :], turns[:, :], 12582912.0, None, ALU.add))
                link(nc.vector.tensor_scalar(turns[:, :], turns[:, :], -12582912.0, None, ALU.add))
                link(nc.vector.scalar_tensor_tensor(angle[:, :], turns[:, :], -TWO_PI[0], pos[:, :], ALU.mult, ALU.add))
                link(nc.vector.scalar_tensor_tensor(angle[:, :], turns[:, :], -TWO_PI[1], angle[:, :], ALU.mult, ALU.add))
                link(nc.vector.scalar_tensor_tensor(angle[:, :], turns[:, :], -TWO_PI[2], angle[:, :], ALU.mult, ALU.add))
                link(nc.vector.tensor_scalar(angle[:, :], angle[:, :], 3.1415925, -3.1415925, ALU.min, ALU.max))
                link(nc.vector.tensor_scalar(angle_c[:, :], angle[:, :], -1.0, None, ALU.mult))
                link(nc.vector.tensor_tensor(angle_c[:, :], angle_c[:, :], angle[:, :], ALU.max))
                nc.vector.tensor_scalar(angle_c[:, :], angle_c[:, :], -1.0, 1.5707963267948966, ALU.mult,
                                        ALU.add).then_inc(angles_ready, 1)

            def condition():
                dve.wait_ge(ld_cond, 16)
                nc.vector.tensor_copy(cond_wide[:, 0, :, :], cond[:, :].rearrange("p (b a) -> p b a", a=1).to_broadcast([128, B, 128]))
                dve.wait_ge(cond_tanh, 1)
                link(nc.vector.scalar_tensor_tensor(cond_silu[:, :], cond_t[:, :], 1.0, cond[:, :], ALU.add, ALU.mult))
                link(nc.vector.tensor_scalar(cond_silu[:, :], cond_silu[:, :], 0.5, None, ALU.mult))
                nc.vector.tensor_copy(cond_wide[:, 1, :, :], cond_silu[:, :].rearrange("p (b a) -> p b a", a=1)
                                      .to_broadcast([128, B, 128])).then_inc(cond_ready, 1)

            def spread_angles():
                dve.wait_ge(sines_ready, 1)
                last = None
                for wide, three in ((sin_w, sin3), (cos_w, cos3)):
                    for b in range(B):
                        to = wide[:, b, :, :].rearrange("p (i t) (c h) -> p i t c h", i=2, h=H)
                        for i in range(2):
                            last = nc.vector.tensor_copy(
                                to[:, i, :, :, :],
                                three[:, b, :, :].rearrange("p t (c a) -> p t c a", a=1).to_broadcast([128, TT, 3, H]))
                link(last)

            def maxima(tick, r):
                it = max_tick(tick, None)
                if it is None:
                    return
                a, g, qt, t = it
                l, b = att(a)
                i = R * t + r
                G = t // TT
                dve.wait_ge(smax_full, i + 1)
                ins = nc.vector.tensor_reduce(nmax[:, G % 2, R * qt + r:R * qt + r + 1],
                                              smax[i % MAX_BANKS][:, 0:max_keys(l, qt)], AX.X, ALU.max, negate=True)
                ins.then_inc(smax_free, 1)
                if qt == TT - 1 and r == R - 1:
                    dve.wait_ge(smax_free, i + 1)
                    if G >= 2:
                        wait_full(dve, "max_rows", G - 2)
                    m = nmax[:, G % 2, :]
                    rr = nrest[:, G % 2, :]
                    part = [nmax_parts[:, G % 2, :, k, :] for k in range(3)]
                    m3 = m.rearrange("p (t r) -> p t r", r=R)
                    rr3 = rr.rearrange("p (t r) -> p t r", r=R)
                    link(nc.vector.tensor_copy(part[0], m3))
                    link(nc.vector.tensor_tensor(rr3, m3, part[0], ALU.subtract))
                    link(nc.vector.tensor_copy(part[1], rr3))
                    nc.vector.tensor_tensor(part[2], rr3, part[1], ALU.subtract).then_inc(nmax_ready, 1)

            def update(use, w):
                _, l, b, h = use
                if h == 0 and (l, b, w) in BIASED:
                    dve.wait_ge(xb_ready, BIASED.index((l, b, w)) + 1)
                wait_full(dve, *use)
                half = x[b][:, 2 * h:2 * h + 2, :]
                nc.vector.tensor_tensor(half, bank(*use)[:, 2 * D * h:2 * D * h + 2 * D].rearrange("p (t f) -> p t f", f=D),
                                        half, ALU.add).then_inc(free(*use), 1)
                if l + w < LAYERS:
                    wait_taken(dve, *use)
                    for t in (2 * h, 2 * h + 1):
                        last = nc.vector.bn_stats(bn[:, t, :], x[b][:, t, :])
                    if h:
                        link(last)
                        variance(l + w)

            def statistics(l, b):
                for t in range(TT):
                    last = nc.vector.bn_stats(bn[:, t, :], x[b][:, t, :])
                link(last)
                variance(l)

            def variance(l):
                for t in range(TT):
                    last = nc.vector.bn_aggr(mv[:, t, :], bn[:, t, :])
                link(last)
                if l == 0:
                    link(nc.vector.tensor_tensor(msq[:, :], mv[:, :, 0], mv[:, :, 0], ALU.mult))
                    nc.vector.scalar_tensor_tensor(ve[:, :], msq[:, :], EPS[l], mv[:, :, 1], ALU.add,
                                                   ALU.add).then_inc(var_ready, 1)
                else:
                    nc.vector.tensor_scalar(ve[:, :], mv[:, :, 1], EPS[l], None, ALU.add).then_inc(var_ready, 1)

            def stage(s):
                if s[0] == "modcol":
                    l = s[1]
                    wait_full(dve, *s)
                    if l == 0:
                        dve.wait_ge(ld_small, 16 * 4)
                    m = mod[:, l, :, :, :]
                    nc.vector.tensor_tensor(
                        m.rearrange("p w c b -> p (w c) b"), bank(*s)[:, 0:8].rearrange("p (c b) -> p c b", b=B),
                        col[:, MODB0 + 4 * l:MODB0 + 4 * l + 4].rearrange("p (c a) -> p c a", a=1).to_broadcast([128, 4, B]),
                        ALU.add).then_inc(free(*s), 1)
                    wait_taken(dve, *s)
                    nw = col[:, NW0 + 2 * l:NW0 + 2 * l + 2].rearrange("p (c a) -> p c a", a=1).to_broadcast([128, 2, B])
                    nb = col[:, NB0 + 2 * l:NB0 + 2 * l + 2].rearrange("p (c a) -> p c a", a=1).to_broadcast([128, 2, B])
                    nc.vector.scalar_tensor_tensor(mod_scale[:, l, :, :], m[:, :, 1, :], 1.0, nw, ALU.add, ALU.mult)
                    link(nc.vector.scalar_tensor_tensor(mod_shift[:, l, :, :], m[:, :, 1, :], 1.0, nb, ALU.add, ALU.mult))
                    nc.vector.tensor_tensor(mod_shift[:, l, :, :], mod_shift[:, l, :, :], m[:, :, 0, :],
                                            ALU.add).then_inc(mod_ready, 1)
                elif s[0] == "gate":
                    l = s[1]
                    wait_full(dve, *s)
                    if l:
                        dve.wait_ge(gated_ready, l)
                    g0 = (GATE_ROW0 + 2 * l) * D
                    for b in range(B):
                        last = nc.vector.tensor_tensor(
                            gates[:, :, b, :], bank(*s)[:, :].rearrange("p (w b f) -> p w b f", w=2, b=B)[:, :, b, :],
                            row[:, g0:g0 + 2 * D].rearrange("p (w f) -> p w f", f=D), ALU.add)
                    last.then_inc(free(*s), 1)
                elif s[0] == "stats":
                    dve.wait_ge(ld_x[s[1]], 16)
                    statistics(0, s[1])
                elif s[0] == "angles":
                    angles()
                elif s[0] == "spread":
                    spread_angles()
                elif s[0] == "condition":
                    condition()
                elif s[0] == "norm":
                    l, b, w = s[1:]
                    n = NORMS[s[1:]]
                    dve.wait_ge(rstd_ready, n + 1)
                    if n:
                        prev = [h for h, k in HTS.items() if k == n - 1][0]
                        wait_full(dve, "hT", *prev)
                    for t in range(TT):
                        if l == 0:
                            last = nc.vector.tensor_scalar(xn[:, t, :], x[b][:, t, :], rstd[:, t:t + 1], None, ALU.mult)
                        else:
                            last = nc.vector.tensor_scalar(xn[:, t, :], x[b][:, t, :], mv[:, t, 0:1], rstd[:, t:t + 1],
                                                           ALU.subtract, ALU.mult)
                        last.then_inc(xn_ready, 1)
                elif s[0] == "qk_scale":
                    wait_taken(dve, "q_rows", *s[1:])
                    wait_taken(dve, "k_rows", *s[1:])
                    sq = squares_of[s[2]].rearrange("p i (t d h) -> p (i t) h d", d=HD, h=H)
                    link(nc.vector.tensor_reduce(ss[:, :].rearrange("p (c h) -> p c h", h=H), sq, AX.X, ALU.add))
                    link(nc.vector.tensor_scalar(ss[:, :], ss[:, :], 1.0 / HD, EPS[0], ALU.mult, ALU.add))
                    bits = qk_rs[:, :].bitcast(i32)
                    link(nc.vector.tensor_scalar(bits, ss[:, :].bitcast(i32), 1, None, ALU.logical_shift_right))
                    link(nc.vector.tensor_scalar(bits, bits, -1.0, float(0x5F3759DF), ALU.mult, ALU.add))
                    link(nc.vector.tensor_scalar(ss[:, :], ss[:, :], -0.5, None, ALU.mult))
                    for _ in range(NEWTON_STEPS):
                        link(nc.vector.tensor_tensor(newton[:, :], qk_rs[:, :], qk_rs[:, :], ALU.mult))
                        link(nc.vector.tensor_tensor(newton[:, :], newton[:, :], ss[:, :], ALU.mult))
                        link(nc.vector.scalar_tensor_tensor(qk_rs[:, :], newton[:, :], 1.5, qk_rs[:, :], ALU.add, ALU.mult))
                    for i in range(2):
                        rs = qk_rs[:, 64 * i:64 * i + 64].rearrange("p (t a h) -> p t a h", a=1, h=H)
                        rows = rows_of[s[2]][:, i, :].rearrange("p (t d h) -> p t d h", d=HD, h=H)
                        last = nc.vector.tensor_tensor(rows, rows, rs.to_broadcast([128, TT, HD, H]), ALU.mult)
                    link(last)
                    for i in range(2):
                        w = row[:, QKW0 + D * i:QKW0 + D * i + D].rearrange("p (a c) -> p a c", a=1)
                        rows = rows_of[s[2]][:, i, :].rearrange("p (t c) -> p t c", c=D)
                        last = nc.vector.tensor_tensor(rows, rows, w.to_broadcast([128, TT, D]), ALU.mult)
                    link(last)
                elif s[0] == "rope":
                    b = s[2]
                    pairs = rows_of[b].rearrange("p i (t e f h) -> p (i t) e f h", e=HD // 2, f=2, h=H)
                    even, odd = pairs[:, :, 0:3, 0, :], pairs[:, :, 0:3, 1, :]
                    cw = cos_w[:, b, :, :].rearrange("p c (e h) -> p c e h", h=H)
                    sw = sin_w[:, b, :, :].rearrange("p c (e h) -> p c e h", h=H)
                    n = 2 * TT * 3 * H
                    flat = hidden[:, :, :].rearrange("p i n -> p (i n)")
                    ec, os, es, oc = [flat[:, k * n:(k + 1) * n].rearrange("p (c e h) -> p c e h", e=3, h=H) for k in range(4)]
                    nc.vector.tensor_tensor(ec, even, cw, ALU.mult)
                    nc.vector.tensor_tensor(os, odd, sw, ALU.mult)
                    nc.vector.tensor_tensor(es, even, sw, ALU.mult)
                    link(nc.vector.tensor_tensor(oc, odd, cw, ALU.mult))
                    nc.vector.tensor_tensor(even, ec, os, ALU.subtract)
                    nc.vector.tensor_tensor(odd, es, oc, ALU.add).then_inc(qk_ready, 1)
                elif s[0] in ("q", "k"):
                    i = int(s[0] == "k")
                    dve.wait_ge(hi_ready, 2 * (s[1] * B + s[2]) + i + 1)
                    nc.vector.tensor_tensor(rest[i], bank(*s)[:, :], parts[i][:, 0, :],
                                            ALU.subtract).then_inc(free(*s), 1)
                elif s[0] in ("q_mid", "k_mid") and s[1:] == (0, 0):
                    i = int(s[0] == "k_mid")
                    dve.wait_ge(mid_ready, i + 1)
                    nc.vector.tensor_tensor(parts[i][:, 2, :], rest[i], parts[i][:, 1, :],
                                            ALU.subtract).then_inc(lo_ready, 1)
                elif s[0] == "fold":
                    G = s[1]
                    a, g = divmod(G, GROUPS)
                    wait_full(dve, *s)
                    if g == 0 and a:
                        wait_full(dve, "oT", *att(a - 1))
                    if G:
                        wait_taken(dve, "fold", G - 1)
                    o = bank(*s)[:, :].rearrange("p (t r c) -> p t r c", r=R, c=VW)
                    link(nc.vector.reciprocal(rden[:, :, :], o[:, :, :, HD]))
                    nc.vector.tensor_tensor(
                        o_rows[:, :, R * HD * g:R * HD * (g + 1)].rearrange("p t (r d) -> p t r d", d=HD),
                        o[:, :, :, 0:HD], rden[:, :, :].rearrange("p t (r a) -> p t r a", a=1).to_broadcast([128, TT, R, HD]),
                        ALU.mult).then_inc(free(*s), 1)
                elif s[0] in ("out", "ssm_out"):
                    for h in range(2):
                        update((*s, h), 0)
                elif s[0] == "down" and s[3] % 2:
                    update((*s[:3], s[3] // 2), 1)
                elif s[0] == "swiglu":
                    k = hid_rows(0, s[3])
                    dve.wait_ge(tanh_ready, s[2] * HID_TILES[0] + s[3] + 1)
                    nc.vector.scalar_tensor_tensor(tanh_a[0:k, :], tanh_a[0:k, :], 1.0, bank("gate_half", *s[1:])[0:k, :],
                                                   ALU.add, ALU.mult).then_inc(free("gate_half", *s[1:]), 1)
                    wait_taken(dve, "gate_half", *s[1:])
                    wait_full(dve, "up_half", *s[1:])
                    nc.vector.scalar_tensor_tensor(hidden[0:k, s[3], :], tanh_a[0:k, :], 0.5, bank("up_half", *s[1:])[0:k, :],
                                                   ALU.mult, ALU.mult).then_inc(free("up_half", *s[1:]), 1)

            for p in range(LAST_POINT):
                tick, q = divmod(p, Q)
                maxima(tick, q)
                for s in PLAN.get(p, []):
                    stage(s)

        @block.tensor
        def _(pe):
            mm = nc.tensor.matmul

            def scores_for_max(tick, r):
                it = max_tick(tick, None)
                if it is None:
                    return
                a, g, qt, t = it
                l, b = att(a)
                i = R * t + r
                h = R * g + r
                n = max_keys(l, qt)
                if t % ATT_TICKS == 0 and r == 0:
                    pe.wait_ge(sp_terms[b], 16 * 12 * (l + 1))
                    pe.wait_ge(pool_terms[b], 16 * 6 * (l + 1))
                    if a == 0:
                        pe.wait_ge(consts_ready, 1)
                if i >= MAX_BANKS:
                    pe.wait_ge(smax_free, i - MAX_BANKS + 1)
                last = mm(smax[i % MAX_BANKS][:, 0:n], qx[b][0:TERM_ROWS, h, 128 * qt:128 * qt + 128], kx[b][0:TERM_ROWS, h, 0:n],
                          start=True, stop=not CAUSAL[l])
                if CAUSAL[l]:
                    last = mm(smax[i % MAX_BANKS][:, n - 128:n], ident16[:, :], mask_s[:, :], start=False, stop=True)
                last.then_inc(smax_full, 1)

            def scores_turned(tick, r):
                it = prob_tick(tick)
                if it is None:
                    return
                a, g, kt, v = it
                l, b = att(a)
                j = R * v + r
                h = R * g + r
                G = v // TT
                q0 = first_query(l, kt)
                if v == 0 and r == 0:
                    pe.wait_ge(ones_laid, 16 * B)
                if kt == 0 and r == 0:
                    pe.wait_ge(max_loaded[G % 2], 16 * (G // 2 + 1))
                if j >= ST_BANKS:
                    pe.wait_ge(exp_done, j - ST_BANKS + 1)
                last = mm(st[j % ST_BANKS][:, 0:N - q0], kx[b][0:ROWS, h, 128 * kt:128 * kt + 128], qx[b][0:ROWS, h, q0:N],
                          start=True, stop=not CAUSAL[l])
                if CAUSAL[l]:
                    last = mm(st[j % ST_BANKS][:, 0:128], ident16[:, :], mask_t[:, :], start=False, stop=True)
                last.then_inc(st_full, 1)

            def times_v(tick, q):
                it = pv_tick(tick)
                if it is None:
                    return
                a, g, kt, v = it
                l, b = att(a)
                q0 = first_query(l, kt)
                heads = pv_heads(kt, q)
                if not heads:
                    return
                pe.wait_ge(exp_done, R * v + heads[-1] + 1)
                if kt == 0 and heads[0] == 0:
                    if v:
                        pe.wait_ge(o_ready, v // TT)
                    if g == 0:
                        wait_taken(pe, "v", l, b)
                for r in heads:
                    last = mm(o_acc[VW * r:VW * r + VW, q0:N], vx[b][:, H * kt + R * g + r, :],
                              probs[:, (R * v + r) % 8, 0:N - q0], start=kt == 0, stop=kt == TT - 1)
                if heads[-1] == R - 1:
                    last.then_inc(pv_done, 1)

            def output(s, turned, weight):
                for h in range(2):
                    wait_free(pe, *s, h)
                    for t in (2 * h, 2 * h + 1):
                        last = mm(bank(*s, h)[:, D * t:D * t + D], turned[:, 128 * t:128 * t + 128], weight[:, :],
                                  start=True, stop=True)
                    last.then_inc(full(*s, h), 1)

            def stage(s):
                if s[0] == "modcol":
                    l = s[1]
                    c = cond if l == 0 else cond_silu
                    pe.wait_ge(ld_ada[l], 16)
                    if l == 0:
                        pe.wait_ge(ld_cond, 16)
                    else:
                        pe.wait_ge(cond_ready, 1)
                    wait_free(pe, *s)
                    for k, chunk in enumerate((0, 1, 3, 4)):
                        last = mm(bank(*s)[:, B * k:B * k + B], wada[l][:, chunk, :], c[:, :], start=True, stop=True)
                    last.then_inc(full(*s), 1)
                elif s[0] == "gate":
                    l = s[1]
                    pe.wait_ge(cond_ready, 1)
                    wait_free(pe, *s)
                    for w, chunk in enumerate((2, 5)):
                        for b in range(B):
                            o = D * (B * w + b)
                            last = mm(bank(*s)[:, o:o + D], cond_wide[:, int(l > 0), b, :], wada[l][:, chunk, :],
                                      start=True, stop=True)
                    last.then_inc(full(*s), 1)
                elif s[0] == "max_rows":
                    G = s[1]
                    pe.wait_ge(nmax_ready, G + 1)
                    wait_free(pe, *s)
                    for t in range(TT):
                        last = nc.tensor.transpose(bank(*s)[0:3 * R, 64 * t:64 * t + 64].bitcast(bf16),
                                                   nmax_parts[:, G % 2, t, :, :].rearrange("p k r -> p (k r)"), ident16[:, :])
                    last.then_inc(full(*s), 1)
                elif s[0] == "fold":
                    G = s[1]
                    pe.wait_ge(o_ready, G + 1)
                    wait_free(pe, *s)
                    for t in range(TT):
                        last = nc.tensor.transpose(bank(*s)[:, 128 * t:128 * t + 128], o_sb[:, G % 2, 128 * t:128 * t + 128],
                                                   ident[:, :])
                    last.then_inc(full(*s), 1)
                elif s[0] == "oT":
                    for g in range(GROUPS):
                        wait_taken(pe, "fold", GROUPS * (s[1] * B + s[2]) + g)
                    wait_free(pe, *s)
                    for t in range(TT):
                        last = nc.tensor.transpose(bank(*s)[:, 128 * t:128 * t + 128], o_rows[:, t, :], ident[:, :])
                    last.then_inc(full(*s), 1)
                elif s[0] == "hT":
                    if HTS[s[1:]] == 0:
                        pe.wait_ge(identity_ready, 1)
                    wait_free(pe, *s)
                    for t in range(TT):
                        pe.wait_ge(xn_ready, TT * HTS[s[1:]] + t + 1)
                        last = nc.tensor.transpose(bank(*s)[:, 128 * t:128 * t + 128], xn[:, t, :], ident[:, :])
                    last.then_inc(full(*s), 1)
                elif s[0] == "out":
                    l, b = s[1:]
                    wait_taken(pe, "oT", *s[1:])
                    pe.wait_ge(gated_ready, l + 1)
                    output(s, oT[:, :], wout_g[l][b])
                elif s[0] == "qk_rows":
                    l, b = s[1:]
                    wait_taken(pe, "hT", l, b, 0)
                    pe.wait_ge(ld_qkv[l], 16)
                    for i, name in enumerate(("q_rows", "k_rows")):
                        wait_free(pe, name, l, b)
                        for t in range(TT):
                            last = mm(bank(name, l, b)[:, D * t:D * t + D], hT[:, 128 * t:128 * t + 128], wqkv[l][:, i, :],
                                      start=True, stop=True)
                        last.then_inc(full(name, l, b), 1)
                elif s[0] == "v":
                    l, b = s[1:]
                    wait_taken(pe, "hT", l, b, 0)
                    pe.wait_ge(ld_qkv[l], 16)
                    wait_free(pe, *s)
                    for t in range(TT):
                        last = mm(bank(*s)[:, D * t:D * t + D], hT[:, 128 * t:128 * t + 128], wqkv[l][:, 2, :],
                                  start=True, stop=True)
                    last.then_inc(full(*s), 1)
                elif s[0] in ("q", "k"):
                    l, b = s[1:]
                    i = int(s[0] == "k")
                    wait_free(pe, *s)
                    if l == 0:
                        pe.wait_ge(qk_ready, b + 1)
                        for t in range(TT):
                            last = nc.tensor.transpose(bank(*s)[:, 128 * t:128 * t + 128], rows_of[b][:, i, 128 * t:128 * t + 128],
                                                       ident[:, :])
                    else:
                        wait_taken(pe, "hT", l, b, 0)
                        pe.wait_ge(ld_qkv[l], 16)
                        last = mm(bank(*s)[:, :], wqkv[l][:, i, :], hT[:, :], start=True, stop=True)
                    last.then_inc(full(*s), 1)
                elif s[0] == "swiglu":
                    l, b, i = s[1:]
                    k = hid_rows(0, i)
                    if i == 0:
                        wait_taken(pe, "hT", l, b, 1)
                        pe.wait_ge(ld_w[0], 16 * W_LOADS[0])
                    for w, name in enumerate(("gate_half", "up_half")):
                        wait_free(pe, name, *s[1:])
                        mm(bank(name, *s[1:])[0:k, :], wup0[:, w, 128 * i:128 * i + k], hT[:, :],
                           start=True, stop=True).then_inc(full(name, *s[1:]), 1)
                elif s[0] == "up":
                    l, b = s[1:]
                    wait_taken(pe, "hT", l, b, 1)
                    pe.wait_ge(ld_w[l], 16 * W_LOADS[l])
                    for i in range(HID_TILES[l]):
                        wait_free(pe, *s, i)
                        mm(bank(*s, i)[:, :], wup[l][:, 128 * i:128 * i + 128], hT[:, :],
                           start=True, stop=True).then_inc(full(*s, i), 1)
                elif s[0] == "ssm":
                    wait_taken(pe, "hT", 3, s[2], 0)
                    pe.wait_ge(ld_w[3], 16 * W_LOADS[3])
                    wait_free(pe, *s)
                    mm(bank(*s)[:, :], wssm[:, :], hT[:, :], start=True, stop=True).then_inc(full(*s), 1)
                elif s[0] == "ssm_out":
                    wait_taken(pe, "ssm", 3, s[2])
                    pe.wait_ge(gated_ready, 4)
                    output(s, hidden[:, 0, :], wout_g[3][s[2]])
                elif s[0] == "down":
                    l, b, t = s[1:]
                    use = ("down", l, b, t // 2)
                    if t == 0:
                        for i in range(HID_TILES[l]):
                            wait_taken(pe, "up_half" if l == 0 else "up", l, b, i)
                        pe.wait_ge(gated_ready, l + 1)
                    if t % 2 == 0:
                        wait_free(pe, *use)
                    for i in range(HID_TILES[l]):
                        k = hid_rows(l, i)
                        last = mm(bank(*use)[:, D * t:D * t + D], hidden[0:k, i, 128 * t:128 * t + 128],
                                  wdown_g[l][b][0:k, i, :], start=i == 0, stop=i == HID_TILES[l] - 1)
                    if t % 2:
                        last.then_inc(full(*use), 1)

            for p in range(LAST_POINT):
                tick, q = divmod(p, Q)
                scores_for_max(tick, q)
                scores_turned(tick, q)
                times_v(tick, q)
                for s in PLAN.get(p, []):
                    stage(s)


def kernel(**inputs):
    import numpy as np
    import concourse.bacc as bacc
    from concourse.bass_utils import run_bass_kernel_spmd

    v = {k: np.asarray(a) for k, a in inputs.items()}
    f = np.ascontiguousarray
    turned = np.arange(D).reshape(H, HD).T.reshape(D)
    shared = np.repeat(np.arange(D // R).reshape(GROUPS, 1, HD), R, axis=1).reshape(D)

    qkv0, qkv1 = v["L0_cond_qkv_w"].T, v["L1_cond_Wqkv"]
    wq2, wk2, wv2 = v["L2_cond_wq"].T, v["L2_cond_wk"].T, v["L2_cond_wv"].T
    ada_b = [v["L0_cond_ada_b"], v["L1_cond_bada"], v["L2_cond_bc"], v["L3_cond_ada_b"]]
    one, zero = np.ones(D, np.float32), np.zeros(D, np.float32)
    norm_w = [v["L0_cond_norm1_w"], v["L0_cond_norm2_w"], v["L1_cond_g1"], v["L1_cond_g2"], one, one, one, one]
    norm_b = [zero, zero, v["L1_cond_be1"], v["L1_cond_be2"], zero, zero, zero, zero]
    cols = [b.reshape(6, D)[c] for b in ada_b for c in (0, 1, 3, 4)] + norm_w + norm_b
    cols += [*v["L1_cond_b1"].reshape(4, D), *v["L2_cond_b1"].reshape(4, D), v["L3_cond_ssm_b1"],
             *v["L3_cond_ff_b1"].reshape(2, D)]
    rows = [v["L0_cond_proj_b"], v["L1_cond_bproj"], v["L1_cond_b2"], v["L2_cond_b2"], v["L3_cond_ssm_b2"],
            v["L3_cond_ff_b2"]]
    rows += [b.reshape(6, D)[c] for b in ada_b for c in (2, 5)]
    rows += [np.repeat(v["L0_cond_q_norm_w"], H), np.repeat(v["L0_cond_k_norm_w"], H)]
    arrays = {
        "x": f(v["x"]), "cond": f(v["cond_1024"].T), "pos": f(v["fside_BxSx3_0"]),
        "col_vecs": f(np.stack(cols, axis=1)), "row_vecs": f(np.concatenate(rows)),
        "wqkv0": f(np.concatenate([qkv0[:, :D][:, turned], qkv0[:, D:2 * D][:, turned], qkv0[:, 2 * D:]], axis=1)),
        "wqkv1": f(np.concatenate([qkv1[:, :D][:, turned], qkv1[:, D:2 * D][:, turned], qkv1[:, 2 * D:]], axis=1)),
        "wqkv2": f(np.concatenate([wq2[:, turned], wk2[:, shared][:, turned], wv2[:, shared]], axis=1)),
        "wout0": f(v["L0_cond_proj_w"].T), "wout1": f(v["L1_cond_Wproj"]), "wout2": f(v["L2_cond_wo"].T),
        "wout3": f(v["L3_cond_ssm_w2"]), "wssm": f(v["L3_cond_ssm_w1"]),
        "wup0": f(np.concatenate([v["L0_cond_w1"].T, v["L0_cond_w3"].T], axis=1)), "wup1": f(v["L1_cond_W1"]),
        "wup2": f(v["L2_cond_w1"].T), "wup3": f(v["L3_cond_ff_w1"]),
        "wdown0": f(v["L0_cond_w2"].T), "wdown1": f(v["L1_cond_W2"]), "wdown2": f(v["L2_cond_w2"].T),
        "wdown3": f(v["L3_cond_ff_w2"]),
        "wada0": f(v["L0_cond_ada_w"].T), "wada1": f(v["L1_cond_Wada"]), "wada2": f(v["L2_cond_wc"].T),
        "wada3": f(v["L3_cond_ada_w"]),
    }
    nc = bacc.Bacc("TRN2", target_bir_lowering=False, num_devices=1)
    t_in = {k: nc.dram_tensor(f"in_{k}", a.shape, mybir.dt.float32, kind="ExternalInput").ap() for k, a in arrays.items()}
    out = nc.dram_tensor("out", (B, N, D), mybir.dt.float32, kind="ExternalOutput").ap()
    program(nc, t_in, out)
    r = run_bass_kernel_spmd(nc, [{f"in_{k}": a for k, a in arrays.items()}], core_ids=[0])
    return r.results[0]["out"]
```
